# Optimizing a Trainium2 kernel written in Bass

```python
import numpy as np
import jax
import jax.numpy as jnp

def _softmax(x, axis=-1):
    return jax.nn.softmax(x, axis=axis)

def _gelu(x):
    return jax.nn.gelu(x, approximate=True)

def _silu(x):
    return jax.nn.silu(x)

def _sigmoid(x):
    return jax.nn.sigmoid(x)

def _layernorm(x, axis=-1, eps=1e-05):
    m = jnp.mean(x, axis=axis, keepdims=True)
    v = jnp.var(x, axis=axis, keepdims=True)
    return (x - m) / jnp.sqrt(v + eps)

def _scatter_add(tgt, idx, src, axis=0):
    return tgt.at[idx].add(src)

def _segment_sum(src, seg, n):
    return jax.ops.segment_sum(src, seg, n)
kernel_name = 'mk_gnn_resnorm_d2_gnn_r32_22548a'

def setup_inputs(seed: int=0):
    np.random.seed(seed)
    _w = jnp.asarray

    def _rec_inputs():
        import jax
        import jax.numpy as jnp
        _gk = jax.random.key(seed)
        x = -0.0009044 + 1 * jax.random.normal(jax.random.fold_in(_gk, 1), (3125, 32), jnp.float32)
        src = jax.random.randint(jax.random.fold_in(_gk, 2), (50000,), 0, 3125, jnp.int32)
        dst = jnp.minimum((3125 * jax.random.uniform(jax.random.fold_in(_gk, 3), (50000,)) ** 2.0).astype(jnp.int32), 99999)
        _o = jnp.argsort(dst, stable=True)
        src = src[_o]
        dst = dst[_o]
        edge_attr_16 = 0.000196303 + 1.00016 * jax.random.normal(jax.random.fold_in(_gk, 13), (50000, 16), jnp.float32)
        edge_attr_4 = 0.00109026 + 0.999989 * jax.random.normal(jax.random.fold_in(_gk, 14), (50000, 4), jnp.float32)
        edge_attr_8 = jax.random.uniform(jax.random.fold_in(_gk, 15), (50000, 8), jnp.float32, 0.0, 1)
        return (x, src, dst, edge_attr_16, edge_attr_4, edge_attr_8)
    x, src, dst, edge_attr_16, edge_attr_4, edge_attr_8 = _rec_inputs()

    def _L0_gnn_setup():
        import jax, jax.numpy as jnp
        import numpy as np
        N = 50000
        E = 50000
        D_IN = 32
        D_EF = 16
        D_H = 64
        D_MSG = 32
        D_UP = 32

        def mlp2(h, W1, b1, W2, b2):
            return jax.nn.relu(h @ W1 + b1) @ W2 + b2
        key = jax.random.key(seed)
        ks = jax.random.split(key, 10)
        s = 0.05
        return {'x': jax.random.normal(ks[0], (N, D_IN), dtype=jnp.float32), 'degrees': jax.random.uniform(ks[1], (N, 1), dtype=jnp.float32), 'edge_features': jax.random.normal(ks[2], (E, D_EF), dtype=jnp.float32), 'W1m': jax.random.normal(ks[3], (2 * D_IN + D_EF, D_H), dtype=jnp.float32) * s, 'b1m': jnp.zeros((D_H,), dtype=jnp.float32), 'W2m': jax.random.normal(ks[4], (D_H, D_MSG), dtype=jnp.float32) * s, 'b2m': jnp.zeros((D_MSG,), dtype=jnp.float32), 'W1u': jax.random.normal(ks[5], (D_IN + D_MSG, D_H), dtype=jnp.float32) * s, 'b1u': jnp.zeros((D_H,), dtype=jnp.float32), 'W2u': jax.random.normal(ks[6], (D_H, D_UP), dtype=jnp.float32) * s, 'b2u': jnp.zeros((D_UP,), dtype=jnp.float32), 'edge_index': jax.random.randint(ks[7], (2, E), 0, N, dtype=jnp.int64)}
    _L0_gnn_all = _L0_gnn_setup()
    _L0_gnn_in = {k: v for k, v in _L0_gnn_all.items() if k in ('W1m', 'b1m', 'W2m', 'b2m', 'W1u', 'b1u', 'W2u', 'b2u')}
    del _L0_gnn_all

    def _L1_gnn_setup():
        import jax, jax.numpy as jnp
        import numpy as np
        MUL = 8
        INV_SQRT3 = float(1.0 / np.sqrt(3.0))
        A_SCALAR = float(np.sqrt(1.0 / 128.0))
        A_VECTOR = float(np.sqrt(3.0 / 128.0))
        SQRT2 = float(np.sqrt(2.0))
        N_NODES, N_EDGES, NUM_BASIS, HIDDEN = (50000, 25000, 8, 256)
        WEIGHT_NUMEL = 4 * MUL * MUL
        k = jax.random.split(jax.random.key(seed), 7)
        node_features = jax.random.normal(k[0], (N_NODES, 4 * MUL), jnp.float32)
        edge_src = jax.random.randint(k[1], (N_EDGES,), 0, N_NODES)
        edge_dst = jax.random.randint(k[2], (N_EDGES,), 0, N_NODES)
        edge_sh = jax.random.normal(k[3], (N_EDGES, 4), jnp.float32)
        edge_scalars = jax.random.uniform(k[4], (N_EDGES, NUM_BASIS), jnp.float32)
        fc_w1 = jax.random.normal(k[5], (NUM_BASIS, HIDDEN), jnp.float32)
        fc_w2 = jax.random.normal(k[6], (HIDDEN, WEIGHT_NUMEL), jnp.float32)
        return dict(node_features=node_features, edge_src=edge_src, edge_dst=edge_dst, edge_sh=edge_sh, edge_scalars=edge_scalars, fc_w1=fc_w1, fc_w2=fc_w2)
    _L1_gnn_all = _L1_gnn_setup()
    _L1_gnn_in = {k: v for k, v in _L1_gnn_all.items() if k in ('fc_w1', 'fc_w2')}
    del _L1_gnn_all
    return {'x': x, 'src': src, 'dst': dst, 'edge_attr_16': edge_attr_16, 'edge_attr_4': edge_attr_4, 'edge_attr_8': edge_attr_8, 'L0_gnn_W1m': _L0_gnn_in['W1m'], 'L0_gnn_b1m': _L0_gnn_in['b1m'], 'L0_gnn_W2m': _L0_gnn_in['W2m'], 'L0_gnn_b2m': _L0_gnn_in['b2m'], 'L0_gnn_W1u': _L0_gnn_in['W1u'], 'L0_gnn_b1u': _L0_gnn_in['b1u'], 'L0_gnn_W2u': _L0_gnn_in['W2u'], 'L0_gnn_b2u': _L0_gnn_in['b2u'], 'L1_gnn_fc_w1': _L1_gnn_in['fc_w1'], 'L1_gnn_fc_w2': _L1_gnn_in['fc_w2']}

def reference(x, src, dst, edge_attr_16, edge_attr_4, edge_attr_8, L0_gnn_W1m, L0_gnn_b1m, L0_gnn_W2m, L0_gnn_b2m, L0_gnn_W1u, L0_gnn_b1u, L0_gnn_W2u, L0_gnn_b2u, L1_gnn_fc_w1, L1_gnn_fc_w2):
    import jax
    import jax.numpy as jnp

    def _L0_gnn_ref(x, degrees, edge_features, W1m, b1m, W2m, b2m, W1u, b1u, W2u, b2u, edge_index):
        import jax, jax.numpy as jnp
        import numpy as np
        N = 50000
        E = 50000
        D_IN = 32
        D_EF = 16
        D_H = 64
        D_MSG = 32
        D_UP = 32

        def mlp2(h, W1, b1, W2, b2):
            return jax.nn.relu(h @ W1 + b1) @ W2 + b2
        src = edge_index[0]
        dst = edge_index[1]
        x_i = x[dst]
        x_j = x[src]
        msg_in = jnp.concatenate([x_i, x_j, edge_features], axis=-1)
        msgs = mlp2(msg_in, W1m, b1m, W2m, b2m)
        agg = jax.ops.segment_sum(msgs, dst, num_segments=x.shape[0])
        upd_in = jnp.concatenate([x, agg], axis=-1)
        return mlp2(upd_in, W1u, b1u, W2u, b2u)

    def _L1_gnn_ref(node_features, edge_src, edge_dst, edge_sh, edge_scalars, fc_w1, fc_w2):
        import jax, jax.numpy as jnp
        import numpy as np
        MUL = 8
        INV_SQRT3 = float(1.0 / np.sqrt(3.0))
        A_SCALAR = float(np.sqrt(1.0 / 128.0))
        A_VECTOR = float(np.sqrt(3.0 / 128.0))
        SQRT2 = float(np.sqrt(2.0))
        N_NODES, N_EDGES, NUM_BASIS, HIDDEN = (50000, 25000, 8, 256)
        WEIGHT_NUMEL = 4 * MUL * MUL
        N = node_features.shape[0]
        E = edge_src.shape[0]
        h = jax.nn.relu(edge_scalars @ (fc_w1 * (1.0 / np.sqrt(NUM_BASIS)))) * SQRT2
        w = (h @ (fc_w2 * (1.0 / np.sqrt(HIDDEN)))).reshape(E, 4, MUL, MUL)
        x = node_features[edge_src]
        s1 = x[:, :MUL]
        v1 = x[:, MUL:].reshape(E, MUL, 3)
        s2 = edge_sh[:, 0]
        v2 = edge_sh[:, 1:4]
        out_s = A_SCALAR * (jnp.einsum('eu,euw->ew', s1 * s2[:, None], w[:, 0]) + INV_SQRT3 * jnp.einsum('eui,ei,euw->ew', v1, v2, w[:, 1]))
        out_v = A_VECTOR * INV_SQRT3 * (jnp.einsum('eu,euw,ei->ewi', s1, w[:, 2], v2) + jnp.einsum('eui,euw->ewi', v1 * s2[:, None, None], w[:, 3]))
        edge_features = jnp.concatenate([out_s, out_v.reshape(E, 3 * MUL)], axis=1)
        node_out = jax.ops.segment_sum(edge_features, edge_dst, num_segments=N)
        return node_out * (1.0 / np.sqrt(E / N))
    edge_index = jnp.stack([src, dst])
    deg = jnp.maximum(jax.ops.segment_sum(jnp.ones(dst.shape, jnp.float32), dst, num_segments=3125), 1.0)
    deg_isqrt = deg ** (-0.5)
    x = _layernorm(x + _L0_gnn_ref(x, deg_isqrt[:, None], edge_attr_16, L0_gnn_W1m, L0_gnn_b1m, L0_gnn_W2m, L0_gnn_b2m, L0_gnn_W1u, L0_gnn_b1u, L0_gnn_W2u, L0_gnn_b2u, edge_index), axis=-1)
    x = _layernorm(x + _L1_gnn_ref(x, src, dst, edge_attr_4, edge_attr_8, L1_gnn_fc_w1, L1_gnn_fc_w2), axis=-1)
    return x

_drawn_inputs = setup_inputs


def setup_inputs(seed=0):
    import zlib

    import numpy as np

    out = dict(_drawn_inputs(seed))
    spreads = {'L0_gnn_b1m': (0.0, 0.1),
     'L0_gnn_b2m': (0.0, 0.1),
     'L0_gnn_b1u': (0.0, 0.339),
     'L0_gnn_b2u': (0.0, 0.1)}
    factors = {'edge_attr_16': 3.157}
    for name, (base, spread) in spreads.items():
        noise = np.random.default_rng([zlib.crc32(name.encode()), seed]).standard_normal(out[name].shape)
        drawn = base * np.exp(spread * noise) if base else spread * noise
        out[name] = jnp.asarray(drawn.astype(out[name].dtype))
    for name, factor in factors.items():
        out[name] = (out[name] * factor).astype(out[name].dtype)
    return out
```

```python
from contextlib import ExitStack

import numpy as np
import concourse.bass as bass
from concourse import mybir

ALU = mybir.AluOpType
ACT = mybir.ActivationFunctionType
AX_X = mybir.AxisListType.X
F32 = mybir.dt.float32
BF16 = mybir.dt.bfloat16
I32 = mybir.dt.int32

P = 128
N, D = 3125, 32
E = 50000
TILES = 4
GE = TILES * P
NG = -(-E // GE)
EP = NG * GE
WIN = 128
NO_DST = 1 << 20
OFF_TABLE = 3200
NT = OFF_TABLE + WIN
NB = NT // P
DEF, DEA, DES = 16, 4, 8
DH = 64
HID = 256
MUL = 8
NCH = -(-NT // 512)
SLOTS = 4
LEAD = 2
ROUNDS = (NG - LEAD) // SLOTS
SPLIT = 3
KS = SPLIT * SPLIT * DES
EC = EP // 16
EPS = 1e-5
HSCALE = float(np.sqrt(2.0) / (np.sqrt(DES) * np.sqrt(HID)))
OSCALE = float(1.0 / np.sqrt(E / N))
C_S = float(np.sqrt(1.0 / 128.0)) * HSCALE * OSCALE
C_V = float(np.sqrt(3.0 / 128.0) / np.sqrt(3.0)) * HSCALE * OSCALE
C_S3 = C_S / float(np.sqrt(3.0))

assert LEAD + ROUNDS * SLOTS == NG and N <= OFF_TABLE and NB * P == NT


class Group:

    def __init__(self, p, i, c):
        self.p, self.i, self.c = p, i, c
        self.slot = c % SLOTS

    def back(self, n):
        return Group(self.p, self.i, self.c - n)

    @property
    def at(self):
        return self.i * SLOTS + self.c

    def count(self, more):
        return self.p * NG + self.i * SLOTS + (self.c + 1 + more)

    def filled(self, each):
        uses = len(range(self.slot, NG, SLOTS))
        return self.p * (uses * each) + self.i * each + (self.c // SLOTS + 1) * each


def sweep(eng, p, step, drain):
    for c in range(LEAD):
        step(Group(p, 0, c))
    with eng.Fori(0, ROUNDS) as i:
        for c in range(LEAD, LEAD + SLOTS):
            step(Group(p, i, c))
    drain(Group(p, 0, NG))


def gnn_program(nc, x_t, x_rows, src_g, dst_row, dst_tiles, ef_t, sh_tiles, es_t,
                W1m, b1m, W2m_t, b2m, W1u, b1u, W2u, b2u, fc_w1, fc_w2, out):
    with ExitStack() as ctx:
        def sb(name, shape, dt=F32):
            return ctx.enter_context(nc.sbuf_tensor(name, shape, dt))

        def sem(name):
            return ctx.enter_context(nc.semaphore(name))

        def sems(name):
            return [sem(f"{name}{s}") for s in range(SLOTS)]

        src_table = nc.dram_tensor("src_table", [NT, DH], F32).ap()
        dst_table = nc.dram_tensor("dst_table", [NT, DH], F32).ap()
        x1_table = nc.dram_tensor("x1_table", [NT, D], F32).ap()
        es_stack = nc.dram_tensor("es_stack", [KS, EP], BF16).ap()
        range_rows = nc.dram_tensor("range_rows", [NG, 2], I32).ap()

        upd_hid = sb("upd_hid", [DH + 1, NT])
        xt1 = upd_hid
        upd_in = sb("upd_in", [P, NT])
        sums1 = sb("sums1", [P, NT])
        tables = sb("tables", [P, NB, 2 * DH])
        x_nm = sb("x_nm", [P, NB, D])
        y = sb("y", [P, NB, D])
        yy = sb("yy", [P, NB, D])
        mean = sb("mean", [P, NB])
        var = sb("var", [P, NB])
        std = sb("std", [P, NB])
        rstd = sb("rstd", [P, NB])
        x1 = sb("x1", [P, NB, D])
        out_sb = sb("out_sb", [P, NB, D])
        w_tab = sb("w_tab", [D + 1, 2 * DH])
        w_ef = sb("w_ef", [DEF, DH])
        w_msg_t = sb("w_msg_t", [D, DH + 1])
        w_upd_a = sb("w_upd_a", [D, DH])
        w_upd = sb("w_upd", [P, DH])
        b_upd = sb("b_upd", [DH, 1])
        w_out = sb("w_out", [DH + 1, D])
        w1s = sb("w1s", [KS, HID], BF16)
        w1f = sb("w1f", [DES, HID])
        w1p = [sb(f"w1p{n}", [DES, HID], BF16) for n in range(SPLIT)]
        w2 = sb("w2", [P, 2, HID])
        fold = sb("fold", [P, D])
        iota_i = sb("iota_i", [P, P], I32)
        iota = sb("iota", [P, P])
        part_i = sb("part_i", [P, 1], I32)
        part_m = sb("part_m", [P, 1], I32)
        part = sb("part", [P, 1])
        part_mf = sb("part_mf", [P, 1])
        dst_g = sb("dst_g", [NG, GE], I32)
        dst_in = sb("dst_in", [NG, GE])
        ranges = sb("ranges", [NG, 2], I32)
        range_row = sb("range_row", [1, NG, 2], I32)
        spans = sb("spans", [1, NG])
        span = sb("span", [1, 1], I32)
        span7 = sb("span7", [1, 1], I32)
        sweeps = sb("sweeps", [1, 1], I32)
        range_all = sb("range_all", [P, NG, 2], I32)
        base = sb("base", [P, NG])
        base_at = sb("base_at", [1, NG], I32)
        shift = sb("shift", [P, 1])
        node_of = sb("node_of", [P, NG])
        dst_l = sb("dst_l", [P, NG, TILES], I32)
        rel = sb("rel", [P, NG, TILES])
        neg_rel = sb("neg_rel", [P, NG, TILES])
        es = sb("es", [P, EC])
        esp = [sb(f"esp{n}", [P, EC], BF16) for n in range(SPLIT)]
        sh = sb("sh", [P, NG * TILES, DEA])
        sh8 = sb("sh8", [P, NG * TILES, 2 * DEA])
        src_i = [sb(f"src_i{s}", [P, TILES], I32) for s in range(SLOTS)]
        dst_b = [sb(f"dst_b{s}", [P, GE], I32) for s in range(SLOTS)]
        hot_t = [sb(f"hot_t{s}", [WIN, GE]) for s in range(SLOTS)]
        hot = [sb(f"hot{s}", [P, TILES, WIN]) for s in range(SLOTS)]
        d_win = [sb(f"d_win{s}", [WIN, DH]) for s in range(SLOTS)]
        ef = [sb(f"ef{s}", [DEF, GE]) for s in range(SLOTS)]
        gat0 = [sb(f"gat0{s}", [P, TILES, DH]) for s in range(SLOTS)]
        pre = [sb(f"pre{b}", [P, TILES, DH]) for b in range(2)]
        hid = [sb(f"hid{b}", [P, TILES, DH + 1]) for b in range(2)]
        gat1 = [sb(f"gat1{s}", [P, TILES, D]) for s in range(SLOTS)]
        es_in = [sb(f"es_in{s}", [KS, GE], BF16) for s in range(SLOTS)]
        hid1 = [sb(f"hid1{b}", [P, 2, GE]) for b in range(2)]
        away = sb("away", [P, TILES, WIN])
        fa = sb("fa", [P, TILES, 2 * MUL])
        fv = sb("fv", [P, TILES, 3, MUL])
        vv = sb("vv", [P, TILES, MUL, 3])
        pa = sb("pa", [P, TILES, 2 * MUL * MUL])
        pv = sb("pv", [P, TILES, 4, MUL * MUL])
        rv = sb("rv", [P, TILES, 4, MUL])
        tv = sb("tv", [P, TILES, MUL, 3])
        msg = [sb(f"msg{b}", [P, TILES, D]) for b in range(2)]

        big = [ctx.enter_context(nc.psum_tensor(f"big{n}", [P, 1024], F32)) for n in range(3)]
        small = [ctx.enter_context(nc.psum_tensor(f"small{n}", [P, 512], F32)) for n in range(2)]
        banks = [b[:, 512 * h:512 * h + 512] for b in big for h in range(2)] + [s[:, :] for s in small]
        pre_ps = [big[2][:, 0:TILES * DH], big[2][:, 512:512 + TILES * DH]]
        hid_ps = big[2]
        w_ps = [b[:, :].rearrange("p (t n) -> p t n", t=TILES) for b in big[0:2]]

        x_in, tab_w, upd_w, dst_grouped, dst_by_tile, es_loaded, mlp1_w, sh_loaded = (
            sem(n) for n in ("x_in", "tab_w", "upd_w", "dst_grouped", "dst_by_tile", "es_loaded", "mlp1_w",
                             "sh_loaded"))
        ones_set, iotas, table_ps, table_act, table_dve = (
            sem(n) for n in ("ones_set", "iotas", "table_ps", "table_act", "table_dve"))
        src_table_out, dst_table_out, ranges_set, ranges_out, range_row_in, range_all_in = (
            sem(n) for n in ("src_table_out", "dst_table_out", "ranges_set", "ranges_out", "range_row_in",
                             "range_all_in"))
        sweeps_set, windows_set, es_cast, es_rest, es_parts_out, w1_parts, w1_stacked = (
            sem(n) for n in ("sweeps_set", "windows_set", "es_cast", "es_rest", "es_parts_out", "w1_parts",
                             "w1_stacked"))
        dve_chain = sem("dve_chain")
        window_base, sh_scaled, hot_away, vec_feats, vec_prods, vec_sums, vec_terms = (
            sem(n) for n in ("window_base", "sh_scaled", "hot_away", "vec_feats", "vec_prods", "vec_sums",
                             "vec_terms"))
        scal_feats, indices_seen = sem("scal_feats"), sem("indices_seen")
        src_in, dstb_in, pre_in, gathered0, es_landed, gathered1 = (
            sems(n) for n in ("src_in", "dstb_in", "pre_in", "gathered0", "es_landed", "gathered1"))
        src1_in = sems("src1_in")
        hot_ready, pre_mm, pre_sum, relu0, seg0, added0 = (
            sem(n) for n in ("hot_ready", "pre_mm", "pre_sum", "relu0", "seg0", "added0"))
        upd_mm, upd_w_mm, upd_w_set, upd_relu, y_mm, var_set, std_set, x1_set, x1_out = (
            sem(n) for n in ("upd_mm", "upd_w_mm", "upd_w_set", "upd_relu", "y_mm", "var_set", "std_set", "x1_set",
                             "x1_out"))
        hid_mm, relu1, w_mm, prods, hot1, msgs, seg1, added1 = (
            sem(n) for n in ("hid_mm", "relu1", "w_mm", "prods", "hot1", "msgs", "seg1", "added1"))
        fold_mm, out_set, out_done = (sem(n) for n in ("fold_mm", "out_set", "out_done"))

        block = ctx.enter_context(nc.Block())

        @block.sync
        def _(sp):
            sp.dma_start(xt1[0:D, :], x_t).then_inc(x_in, 16)
            sp.dma_start(w_tab[0:D, 0:DH], W1m[0:D, :]).then_inc(tab_w, 16)
            sp.dma_start(w_tab[0:D, DH:2 * DH], W1m[D:2 * D, :]).then_inc(tab_w, 16)
            sp.dma_start(w_tab[D:D + 1, 0:DH], b1m.rearrange("(a n) -> a n", a=1)).then_inc(tab_w, 16)
            sp.dma_start(dst_g[:, :], dst_row.rearrange("(g e) -> g e", g=NG)).then_inc(dst_grouped, 16)
            sp.dma_start(dst_l[:, :, :].rearrange("p g t -> p (g t)"), dst_tiles).then_inc(dst_by_tile, 16)
            sp.dma_start(w_ef[:, :], W1m[2 * D:2 * D + DEF, :]).then_inc(upd_w, 16)
            sp.dma_start(w_msg_t[:, 0:DH], W2m_t).then_inc(upd_w, 16)
            sp.dma_start(w_msg_t[:, DH:DH + 1], b2m.rearrange("(n a) -> n a", a=1)).then_inc(upd_w, 16)
            sp.dma_start(w_upd_a[:, :], W1u[D:2 * D, :]).then_inc(upd_w, 16)
            sp.dma_start(b_upd[:, :], b1u.rearrange("(n a) -> n a", a=1)).then_inc(upd_w, 16)
            sp.dma_start(w_out[0:DH, :], W2u).then_inc(upd_w, 16)
            sp.dma_start(w_out[DH:DH + 1, :], b2u.rearrange("(a n) -> a n", a=1)).then_inc(upd_w, 16)
            sp.wait_ge(ranges_set, 2)
            sp.dma_start(range_rows, ranges[:, :]).then_inc(ranges_out, 16)
            sp.wait_ge(ranges_out, 16)
            sp.dma_start(range_row[:, :, :], range_rows.rearrange("(a g) r -> a g r", a=1)).then_inc(range_row_in, 16)
            sp.dma_start(range_all[:, :, :].rearrange("p g r -> p (g r)"),
                         range_rows.rearrange("g r -> (g r)").partition_broadcast(P)).then_inc(range_all_in, 16)
            sp.wait_ge(table_act, NCH // 2)
            sp.wait_ge(table_dve, NCH - NCH // 2)
            sp.dma_start(src_table.rearrange("(b p) f -> p b f", p=P), tables[:, :, DH:2 * DH]).then_inc(src_table_out, 16)
            sp.dma_start(dst_table.rearrange("(b p) f -> p b f", p=P), tables[:, :, 0:DH]).then_inc(dst_table_out, 16)
            sp.wait_ge(ones_set, 6)
            sp.dma_start(upd_in[P - D:P, :], x_t).then_inc(upd_w, 16)
            sp.dma_start(w_upd[P - D:P, :], W1u[0:D, :]).then_inc(upd_w, 16)
            sp.dma_start(x_nm[:, :, :].rearrange("p b f -> p (b f)"), x_rows).then_inc(upd_w, 16)
            sp.wait_ge(dst_table_out, 16)
            sp.wait_ge(sweeps_set, 1)
            n_sweeps = sp.value_load(sweeps[0:1, 0:1], min_val=1, max_val=-(-N // WIN))

            def load0(g):
                sp.wait_ge(pre_sum, g.count(0))
                sp.dma_start(src_i[g.slot][:, :], src_g[bass.ds(g.at, 1), :, :].rearrange("a p t -> (a p) t")).then_inc(src_in[g.slot], 16)
                sp.dma_start(dst_b[g.slot][:, :],
                             dst_row[bass.ds(g.at * GE, GE)].partition_broadcast(P)).then_inc(dstb_in[g.slot], 16)
                first = sp.value_load(base_at[0:1, bass.ds(g.at, 1)], min_val=0, max_val=OFF_TABLE)
                sp.dma_start(d_win[g.slot][:, :], dst_table[bass.ds(first, WIN), :]).then_inc(pre_in[g.slot], 16)
                sp.dma_start(ef[g.slot][:, :], ef_t[:, bass.ds(g.at * GE, GE)]).then_inc(pre_in[g.slot], 16)

            with sp.Fori(0, n_sweeps) as p:
                sp.wait_ge(windows_set, p + 1)
                sweep(sp, p, load0, lambda g: None)

            sp.wait_ge(x1_set, 1)
            sp.dma_start(x1_table.rearrange("(b p) f -> p b f", p=P), x1[:, :, :]).then_inc(x1_out, 16)
            sp.wait_ge(es_parts_out, 16 * SPLIT * SPLIT)

            def load1(g):
                sp.wait_ge(msgs, g.count(0))
                sp.dma_start(src_i[g.slot][:, :], src_g[bass.ds(g.at, 1), :, :].rearrange("a p t -> (a p) t")).then_inc(src1_in[g.slot], 16)
                sp.dma_start(es_in[g.slot][:, :], es_stack[:, bass.ds(g.at * GE, GE)]).then_inc(es_landed[g.slot], 16)

            with sp.Fori(0, n_sweeps) as p:
                sweep(sp, p, load1, lambda g: None)

            sp.wait_ge(out_set, 1)
            full = N // P
            sp.dma_start(out[0:full * P, :].rearrange("(b p) f -> p b f", p=P), out_sb[:, 0:full, :]).then_inc(out_done, 16)
            sp.dma_start(out[full * P:N, :], out_sb[0:N - full * P, full, :]).then_inc(out_done, 16)
            sp.wait_ge(out_done, 32)

        @block.gpsimd
        def _(pool):
            pool.iota(iota_i[:, :], [[1, P]], base=0, channel_multiplier=0).then_inc(iotas, 1)
            pool.iota(part_i[:, :], [[0, 1]], base=0, channel_multiplier=1).then_inc(iotas, 1)
            pool.wait_ge(sweeps_set, 1)
            n_sweeps = pool.value_load(sweeps[0:1, 0:1], min_val=1, max_val=-(-N // WIN))
            pool.wait_ge(src_table_out, 16)

            def gather0(g):
                pool.wait_ge(src_in[g.slot], g.filled(16))
                pool.sem_inc(indices_seen, 1)
                for t in range(TILES):
                    pool.indirect_dma_start(
                        out=gat0[g.slot][:, t, :], out_offset=None, in_=src_table,
                        in_offset=bass.IndirectOffsetOnAxis(ap=src_i[g.slot][:, t:t + 1], axis=0),
                    ).then_inc(gathered0[g.slot], 16)

            with pool.Fori(0, n_sweeps) as p:
                sweep(pool, p, gather0, lambda g: None)

            pool.wait_ge(x1_out, 16)

            def gather1(g):
                pool.wait_ge(src1_in[g.slot], g.filled(16))
                pool.sem_inc(indices_seen, 1)
                for t in range(TILES):
                    pool.indirect_dma_start(
                        out=gat1[g.slot][:, t, :], out_offset=None, in_=x1_table,
                        in_offset=bass.IndirectOffsetOnAxis(ap=src_i[g.slot][:, t:t + 1], axis=0),
                    ).then_inc(gathered1[g.slot], 16)

            with pool.Fori(0, n_sweeps) as p:
                sweep(pool, p, gather1, lambda g: None)

        @block.tensor
        def _(pe):
            pe.wait_ge(x_in, 16)
            pe.wait_ge(tab_w, 48)
            pe.wait_ge(ones_set, 2)
            for c in range(NCH):
                for b in range(4 * c, min(4 * c + 4, NB)):
                    k = b - 4 * c
                    mm = pe.matmul(banks[c][:, k * P:(k + 1) * P], xt1[0:D + 1, b * P:(b + 1) * P], w_tab[:, :],
                                   start=True, stop=True)
                mm.then_inc(table_ps, 1)
            pe.wait_ge(upd_w, 16 * 10)
            pe.matmul(banks[7][0:DH + 1, 0:DH], w_msg_t[:, :], w_upd_a[:, :], start=True, stop=True).then_inc(upd_w_mm, 1)
            pe.wait_ge(sweeps_set, 1)
            n_sweeps = pe.value_load(sweeps[0:1, 0:1], min_val=1, max_val=-(-N // WIN))
            pe.wait_ge(table_act, NCH // 2)
            pe.wait_ge(table_dve, NCH - NCH // 2)
            pe.wait_ge(upd_w_set, 1)

            def pre_products(g):
                pe.wait_ge(pre_in[g.slot], g.filled(32))
                pe.wait_ge(hot_ready, g.count(0))
                pe.wait_ge(pre_sum, g.count(SLOTS - 2))
                for t in range(TILES):
                    o = pre_ps[g.slot % 2][:, t * DH:(t + 1) * DH]
                    pe.matmul(o, hot_t[g.slot][:, t * P:(t + 1) * P], d_win[g.slot][:, :], start=True, stop=False)
                    mm = pe.matmul(o, ef[g.slot][:, t * P:(t + 1) * P], w_ef[:, :], start=False, stop=True)
                mm.then_inc(pre_mm, 1)

            def sum0(g):
                pe.wait_ge(relu0, g.count(0))
                pe.wait_ge(added0, g.count(0))
                for t in range(TILES):
                    mm = pe.matmul(small[g.slot % 2][0:DH + 1, 0:WIN], hid[g.slot % 2][:, t, :], hot[g.slot][:, t, :],
                                   start=t == 0, stop=t == TILES - 1)
                mm.then_inc(seg0, 1)

            def step0(g):
                pre_products(g)
                if g.c >= 2:
                    sum0(g.back(2))

            def drain0(g):
                sum0(g.back(2))
                sum0(g.back(1))

            with pe.Fori(0, n_sweeps) as p:
                sweep(pe, p, step0, drain0)

            pe.wait_ge(added0, n_sweeps * NG + 2)
            for c in range(NCH):
                w = min(512, NT - 512 * c)
                pe.matmul(banks[c][0:DH, 0:w], w_upd[:, :], upd_in[:, 512 * c:512 * c + w],
                          start=True, stop=True).then_inc(upd_mm, 1)
            pe.wait_ge(upd_relu, NCH)
            for b in range(NB):
                mm = pe.matmul(small[b // 16][:, (b % 16) * D:(b % 16 + 1) * D], upd_hid[:, b * P:(b + 1) * P],
                               w_out[:, :], start=True, stop=True)
            mm.then_inc(y_mm, 1)

            pe.wait_ge(w1_stacked, 16 * SPLIT * SPLIT)
            pe.wait_ge(mlp1_w, 32)

            def hidden1(g):
                pe.wait_ge(es_landed[g.slot], g.filled(16))
                pe.wait_ge(relu1, g.count(0))
                for c in range(2):
                    mm = pe.matmul(hid_ps[:, c * GE:(c + 1) * GE], w1s[:, c * P:(c + 1) * P], es_in[g.slot][:, :],
                                   start=True, stop=True)
                mm.then_inc(hid_mm, 1)

            def weights1(g):
                pe.wait_ge(relu1, g.count(1))
                pe.wait_ge(prods, g.count(0))
                for t in range(TILES):
                    for c in range(2):
                        mm = pe.matmul(w_ps[g.slot % 2][:, t, :], hid1[g.slot % 2][:, c, t * P:(t + 1) * P],
                                       w2[:, c, :], start=c == 0, stop=c == 1)
                mm.then_inc(w_mm, 1)

            def sum1(g):
                pe.wait_ge(msgs, g.count(SLOTS))
                pe.wait_ge(hot1, g.count(1))
                pe.wait_ge(added1, g.count(0))
                for t in range(TILES):
                    mm = pe.matmul(small[g.slot % 2][t * D:(t + 1) * D, 0:WIN], msg[g.slot % 2][:, t, :],
                                   hot[g.slot][:, t, :], start=True, stop=True)
                mm.then_inc(seg1, 1)

            def step1(g):
                hidden1(g)
                if g.c >= 1:
                    weights1(g.back(1))
                if g.c >= 2:
                    sum1(g.back(2))

            def drain1(g):
                weights1(g.back(1))
                sum1(g.back(2))
                sum1(g.back(1))

            with pe.Fori(0, n_sweeps) as p:
                sweep(pe, p, step1, drain1)

            pe.wait_ge(added1, n_sweeps * NG + 2)
            for b in range(NB):
                mm = pe.matmul(banks[b // 16][:, (b % 16) * D:(b % 16 + 1) * D], sums1[:, b * P:(b + 1) * P],
                               fold[:, :], start=True, stop=True)
            mm.then_inc(fold_mm, 1)

        @block.scalar
        def _(act):
            act.dma_start(es[:, :], es_t).then_inc(es_loaded, 16)
            act.dma_start(w1f[:, :], fc_w1).then_inc(mlp1_w, 16)
            act.dma_start(w2[:, :, :], fc_w2.rearrange("(c p) n -> p c n", c=2)).then_inc(mlp1_w, 16)
            act.dma_start(sh[:, :, :].rearrange("p t k -> p (t k)"), sh_tiles).then_inc(sh_loaded, 16)
            for c in range(1, NCH, 2):
                act.wait_ge(table_ps, c + 1)
                nb = min(4, NB - 4 * c)
                act.activation(tables[:, 4 * c:4 * c + nb, :].rearrange("p b f -> p (b f)"), banks[c][:, 0:nb * P],
                               ACT.Copy).then_inc(table_act, 1)
            act.wait_ge(upd_w_mm, 1)
            act.activation(w_upd[0:DH + 1, :], banks[7][0:DH + 1, 0:DH], ACT.Copy).then_inc(upd_w_set, 1)
            act.wait_ge(es_loaded, 16)
            for n in range(SPLIT):
                if n:
                    act.wait_ge(es_rest, n)
                act.activation(esp[n][:, :], es[:, :], ACT.Copy).then_inc(es_cast, 1)
            act.wait_ge(es_cast, SPLIT)
            for j in range(SPLIT):
                for i in range(SPLIT):
                    r = (j * SPLIT + i) * DES
                    act.dma_start(es_stack[r:r + DES, :].rearrange("f (c e) -> (f c) e", e=EC),
                                  esp[i][:, :]).then_inc(es_parts_out, 16)
            act.wait_ge(w1_parts, 3)
            for j in range(SPLIT):
                for i in range(SPLIT):
                    r = (j * SPLIT + i) * DES
                    act.dma_start(w1s[r:r + DES, :], w1p[j][:, :]).then_inc(w1_stacked, 16)
            act.wait_ge(sh_loaded, 16)
            act.activation(sh8[:, :, 0:1], sh[:, :, 0:1], ACT.Copy, scale=C_S).then_inc(sh_scaled, 1)
            act.activation(sh8[:, :, 1:DEA], sh[:, :, 1:DEA], ACT.Copy, scale=C_S3).then_inc(sh_scaled, 1)
            act.activation(sh8[:, :, DEA:2 * DEA], sh[:, :, :], ACT.Copy, scale=C_V).then_inc(sh_scaled, 1)
            act.wait_ge(sweeps_set, 1)
            n_sweeps = act.value_load(sweeps[0:1, 0:1], min_val=1, max_val=-(-N // WIN))

            def relu_0(g):
                act.wait_ge(pre_sum, g.count(SLOTS))
                act.wait_ge(seg0, g.count(0))
                act.activation(hid[g.slot % 2][:, :, 0:DH], pre[g.slot % 2][:, :, :], ACT.Relu).then_inc(relu0, 1)

            with act.Fori(0, n_sweeps) as p:
                sweep(act, p, relu_0, lambda g: None)

            for c in range(NCH):
                w = min(512, NT - 512 * c)
                act.wait_ge(upd_mm, c + 1)
                act.activation(upd_hid[0:DH, 512 * c:512 * c + w], banks[c][0:DH, 0:w], ACT.Relu,
                               bias=b_upd[:, :]).then_inc(upd_relu, 1)
            act.wait_ge(var_set, 1)
            act.activation(std[:, :], var[:, :], ACT.Sqrt).then_inc(std_set, 1)

            def relu_1(g):
                act.wait_ge(hid_mm, g.count(0))
                act.wait_ge(w_mm, g.count(0))
                act.activation(hid1[g.slot % 2][:, :, :].rearrange("p c e -> p (c e)"), hid_ps[:, :],
                               ACT.Relu).then_inc(relu1, 1)

            def hot_1(g):
                act.wait_ge(seg1, g.count(0))
                act.wait_ge(hot1, g.count(0))
                for t in range(TILES):
                    last = act.activation(away[:, t, :], iota[:, :], ACT.Square,
                                          bias=neg_rel[:, bass.ds(g.at, 1), t:t + 1].rearrange("p a b -> p (a b)"))
                last.then_inc(hot_away, 1)
                act.wait_ge(hot_away, g.count(0))
                act.activation(hot[g.slot][:, :, :], away[:, :, :], ACT.Relu, scale=-1.0, bias=1.0).then_inc(hot1, 1)

            def step1(g):
                relu_1(g)
                hot_1(g)

            with act.Fori(0, n_sweeps) as p:
                act.wait_ge(windows_set, n_sweeps + p + 1)
                sweep(act, p, step1, lambda g: None)

            act.wait_ge(var_set, 2)
            act.activation(std[:, :], var[:, :], ACT.Sqrt).then_inc(std_set, 1)

        @block.vector
        def _(dve):
            done = [0]

            def link(ins):
                done[0] += 1
                ins.then_inc(dve_chain, 1)
                dve.wait_ge(dve_chain, done[0])

            dve.memset(xt1[D:D + 1, :], 1.0).then_inc(ones_set, 1)
            dve.memset(w_tab[D:D + 1, DH:2 * DH], 0.0).then_inc(ones_set, 1)
            dve.wait_ge(dst_grouped, 16)
            dve.tensor_reduce(ranges[:, 0:1], dst_g[:, :], AX_X, ALU.min).then_inc(ranges_set, 1)
            link(dve.scalar_tensor_tensor(out=dst_in[:, :], in0=dst_g[:, :], scalar=float(NO_DST), in1=dst_g[:, :],
                                          op0=ALU.is_lt, op1=ALU.mult))
            dve.tensor_reduce(ranges[:, 1:2], dst_in[:, :], AX_X, ALU.max).then_inc(ranges_set, 1)
            dve.memset(upd_in[:, :], 0.0).then_inc(ones_set, 1)
            dve.memset(w_upd[:, :], 0.0).then_inc(ones_set, 1)
            dve.memset(upd_hid[DH:DH + 1, :], 1.0).then_inc(ones_set, 1)
            dve.memset(sums1[:, :], 0.0).then_inc(ones_set, 1)
            for b in range(2):
                link(dve.memset(hid[b][:, :, :], 1.0))
            for c in range(0, NCH, 2):
                dve.wait_ge(table_ps, c + 1)
                nb = min(4, NB - 4 * c)
                dve.tensor_copy(tables[:, 4 * c:4 * c + nb, :].rearrange("p b f -> p (b f)"),
                                banks[c][:, 0:nb * P]).then_inc(table_dve, 1)
            dve.wait_ge(range_row_in, 16)
            link(dve.tensor_tensor(spans[:, :], range_row[:, :, 1], range_row[:, :, 0], ALU.subtract))
            link(dve.tensor_reduce(span[:, :], spans[:, :], AX_X, ALU.max))
            link(dve.tensor_scalar(span7[:, :], span[:, :], WIN.bit_length() - 1, None, ALU.arith_shift_right))
            dve.tensor_scalar(sweeps[:, :], span7[:, :], 1.0, None, ALU.add).then_inc(sweeps_set, 1)
            dve.wait_ge(iotas, 2)
            dve.tensor_copy(iota[:, :], iota_i[:, :])
            dve.tensor_copy(part[:, :], part_i[:, :])
            link(dve.tensor_scalar(part_m[:, :], part_i[:, :], D - 1, None, ALU.bitwise_and))
            link(dve.tensor_copy(part_mf[:, :], part_m[:, :]))
            dve.wait_ge(range_all_in, 16)
            dve.wait_ge(dst_by_tile, 16)

            dve.tensor_scalar(fold[:, :], iota[:, 0:D], part_mf[:, 0:1], None, ALU.is_equal).then_inc(dve_chain, 1)
            done[0] += 1
            link(dve.memset(shift[:, :], 0.0))
            for n in range(SPLIT - 1):
                dve.wait_ge(es_cast, n + 1)
                dve.tensor_tensor(es[:, :], es[:, :], esp[n][:, :], ALU.subtract).then_inc(es_rest, 1)
            dve.wait_ge(mlp1_w, 32)
            for n in range(SPLIT):
                dve.tensor_copy(w1p[n][:, :], w1f[:, :]).then_inc(w1_parts, 1)
                if n < SPLIT - 1:
                    dve.wait_ge(w1_parts, n + 1)
                    link(dve.tensor_tensor(w1f[:, :], w1f[:, :], w1p[n][:, :], ALU.subtract))
            for s, n in ((pre_sum, SLOTS), (added0, 2), (seg0, 2), (relu1, 1), (prods, 2), (msgs, SLOTS),
                         (added1, 2), (w_mm, 2), (seg1, SLOTS), (hot1, 1)):
                dve.sem_inc(s, n)
            n_sweeps = dve.value_load(sweeps[0:1, 0:1], min_val=1, max_val=-(-N // WIN))

            def set_windows(sweep_no):
                dve.tensor_scalar(base[:, :], range_all[:, :, 0], shift[:, 0:1], None, ALU.add).then_inc(window_base, 1)
                dve.wait_ge(window_base, sweep_no + 1)
                dve.tensor_scalar(node_of[:, :], base[:, :], part[:, 0:1], None, ALU.add)
                dve.tensor_scalar(base_at[:, :], base[0:1, :], float(OFF_TABLE), None, ALU.min)
                first = base[:, :, None].to_broadcast([P, NG, TILES])
                dve.tensor_tensor(rel[:, :, :], dst_l[:, :, :], first, ALU.subtract)
                dve.tensor_tensor(neg_rel[:, :, :], first, dst_l[:, :, :], ALU.subtract)
                dve.tensor_scalar(shift[:, :], shift[:, :], float(WIN), None, ALU.add).then_inc(windows_set, 1)
                dve.wait_ge(windows_set, sweep_no + 1)

            def one_hots(g):
                dve.wait_ge(dstb_in[g.slot], g.filled(16))
                dve.tensor_scalar(hot_t[g.slot][:, :], dst_b[g.slot][:, :], node_of[:, bass.ds(g.at, 1)], None, ALU.is_equal)
                for t in range(TILES):
                    last = dve.tensor_scalar(hot[g.slot][:, t, :], iota[:, :],
                                             rel[:, bass.ds(g.at, 1), t:t + 1].rearrange("p a b -> p (a b)"), None,
                                             ALU.is_equal)
                last.then_inc(hot_ready, 1)

            def sum_pre(g):
                dve.wait_ge(gathered0[g.slot], g.filled(16 * TILES))
                dve.wait_ge(pre_mm, g.count(0))
                dve.tensor_tensor(pre[g.slot % 2][:, :, :].rearrange("p t f -> p (t f)"), pre_ps[g.slot % 2],
                                  gat0[g.slot][:, :, :].rearrange("p t f -> p (t f)"), ALU.add).then_inc(pre_sum, 1)

            def add_to_nodes(g, acc, rows, summed, credit, added):
                first = dve.value_load(base_at[0:1, bass.ds(g.at, 1)], min_val=0, max_val=OFF_TABLE)
                dve.wait_ge(summed, g.count(credit))
                dve.wait_ge(added, g.count(1))
                there = acc[0:rows, bass.ds(first, WIN)]
                dve.tensor_tensor(there, there, small[g.slot % 2][0:rows, 0:WIN], ALU.add).then_inc(added, 1)

            def step0(g):
                one_hots(g)
                if g.c >= 2:
                    add_to_nodes(g.back(2), upd_in, DH + 1, seg0, 2, added0)
                if g.c >= 1:
                    sum_pre(g.back(1))

            def drain0(g):
                add_to_nodes(g.back(2), upd_in, DH + 1, seg0, 2, added0)
                sum_pre(g.back(1))
                add_to_nodes(g.back(1), upd_in, DH + 1, seg0, 2, added0)

            with dve.Fori(0, n_sweeps) as p:
                set_windows(p)
                sweep(dve, p, step0, drain0)

            def layernorm(src, res, normed, turn):
                flat = y[:, :, :].rearrange("p b f -> p (b f)")
                r = res[:, :, :].rearrange("p b f -> p (b f)")
                dve.tensor_tensor(flat[:, 0:512], src[0][:, 0:512], r[:, 0:512], ALU.add)
                link(dve.tensor_tensor(flat[:, 512:NB * D], src[1][:, 0:NB * D - 512], r[:, 512:NB * D], ALU.add))
                link(dve.tensor_reduce(mean[:, :], y[:, :, :], AX_X, ALU.add))
                link(dve.tensor_scalar(mean[:, :], mean[:, :], 1.0 / D, None, ALU.mult))
                link(dve.tensor_tensor(yy[:, :, :], y[:, :, :], mean[:, :, None].to_broadcast([P, NB, D]), ALU.subtract))
                link(dve.tensor_tensor(y[:, :, :], yy[:, :, :], yy[:, :, :], ALU.mult))
                link(dve.tensor_reduce(var[:, :], y[:, :, :], AX_X, ALU.add))
                dve.tensor_scalar(var[:, :], var[:, :], 1.0 / D, EPS, ALU.mult, ALU.add).then_inc(var_set, 1)
                dve.wait_ge(std_set, turn)
                link(dve.reciprocal(rstd[:, :], std[:, :]))
                return dve.tensor_tensor(normed[:, :, :], yy[:, :, :], rstd[:, :, None].to_broadcast([P, NB, D]), ALU.mult)

            dve.wait_ge(y_mm, 1)
            layernorm(small, x_nm, x1, 1).then_inc(x1_set, 1)
            link(dve.memset(shift[:, :], 0.0))
            dve.wait_ge(sh_scaled, 3)

            def features(g):
                dve.wait_ge(gathered1[g.slot], g.filled(16 * TILES))
                s1 = gat1[g.slot][:, :, 0:MUL]
                v1 = gat1[g.slot][:, :, MUL:D].rearrange("p t (u i) -> p t u i", i=3)
                h = sh8[:, bass.ds(g.at * TILES, TILES), :]
                dve.tensor_tensor(vv[:, :, :, :], v1, h[:, :, None, 1:DEA].to_broadcast([P, TILES, MUL, 3]),
                                  ALU.mult).then_inc(vec_feats, 1)
                dve.tensor_tensor(fa[:, :, 0:MUL], s1, h[:, :, 0:1].to_broadcast([P, TILES, MUL]), ALU.mult)
                dve.tensor_tensor(fv[:, :, :, :].rearrange("p t i u -> p t (i u)"), v1.rearrange("p t u i -> p t i u"),
                                  h[:, :, DEA:DEA + 1].to_broadcast([P, TILES, 3 * MUL]), ALU.mult)
                dve.wait_ge(vec_feats, g.count(0))
                dve.tensor_reduce(fa[:, :, MUL:2 * MUL], vv[:, :, :, :], AX_X, ALU.add).then_inc(scal_feats, 1)
                return s1, h

            def messages(g):
                s1, h = features(g)
                w = w_ps[g.slot % 2]
                dve.wait_ge(w_mm, g.count(2))
                dve.tensor_tensor(pv[:, :, 0, :].rearrange("p t (u w) -> p t u w", w=MUL),
                                  w[:, :, 128:192].rearrange("p t (u w) -> p t u w", w=MUL),
                                  s1[:, :, :, None].to_broadcast([P, TILES, MUL, MUL]), ALU.mult)
                dve.wait_ge(scal_feats, g.count(0))
                dve.tensor_tensor(pv[:, :, 1:4, :].rearrange("p t i (u w) -> p t i u w", w=MUL),
                                  w[:, :, None, 192:256].rearrange("p t i (u w) -> p t i u w", w=MUL)
                                  .to_broadcast([P, TILES, 3, MUL, MUL]),
                                  fv[:, :, :, :, None].to_broadcast([P, TILES, 3, MUL, MUL]), ALU.mult).then_inc(vec_prods, 1)
                dve.tensor_tensor(pa[:, :, :].rearrange("p t (u w) -> p t u w", w=MUL),
                                  w[:, :, 0:128].rearrange("p t (u w) -> p t u w", w=MUL),
                                  fa[:, :, :, None].to_broadcast([P, TILES, 2 * MUL, MUL]), ALU.mult).then_inc(prods, 1)
                dve.wait_ge(vec_prods, g.count(0))
                dve.tensor_reduce(rv[:, :, :, :], pv[:, :, :, :].rearrange("p t j (u w) -> p t j w u", w=MUL), AX_X,
                                  ALU.add).then_inc(vec_sums, 1)
                dve.wait_ge(prods, g.count(2))
                dve.tensor_reduce(msg[g.slot % 2][:, :, 0:MUL], pa[:, :, :].rearrange("p t (u w) -> p t w u", w=MUL),
                                  AX_X, ALU.add)
                dve.wait_ge(vec_sums, g.count(0))
                dve.tensor_tensor(tv[:, :, :, :], rv[:, :, 0, :, None].to_broadcast([P, TILES, MUL, 3]),
                                  h[:, :, None, DEA + 1:2 * DEA].to_broadcast([P, TILES, MUL, 3]), ALU.mult).then_inc(vec_terms, 1)
                dve.wait_ge(vec_terms, g.count(0))
                dve.tensor_tensor(msg[g.slot % 2][:, :, MUL:D].rearrange("p t (w i) -> p t w i", i=3), tv[:, :, :, :],
                                  rv[:, :, 1:4, :].rearrange("p t i w -> p t w i"), ALU.add).then_inc(msgs, 1)

            def step1(g):
                messages(g)
                if g.c >= 1:
                    add_to_nodes(g.back(1), sums1, P, seg1, SLOTS, added1)

            def drain1(g):
                add_to_nodes(g.back(1), sums1, P, seg1, SLOTS, added1)

            with dve.Fori(0, n_sweeps) as p:
                set_windows(n_sweeps + p)
                sweep(dve, p, step1, drain1)

            dve.wait_ge(fold_mm, 1)
            layernorm(banks, x1, out_sb, 2).then_inc(out_set, 1)


def kernel(x, src, dst, edge_attr_16, edge_attr_4, edge_attr_8, L0_gnn_W1m, L0_gnn_b1m, L0_gnn_W2m, L0_gnn_b2m,
           L0_gnn_W1u, L0_gnn_b1u, L0_gnn_W2u, L0_gnn_b2u, L1_gnn_fc_w1, L1_gnn_fc_w2):
    import concourse.bacc as bacc
    from concourse.bass_utils import run_bass_kernel_spmd

    def padded(a, rows, fill=0):
        a = np.asarray(a)
        full = np.full((rows,) + a.shape[1:], fill, a.dtype)
        full[:a.shape[0]] = a
        return full

    xp = padded(x, NT)
    dp = padded(dst, EP, NO_DST)
    arrays = {
        "x_t": np.ascontiguousarray(xp.T),
        "x_rows": np.ascontiguousarray(xp.reshape(NB, P, D).transpose(1, 0, 2)).reshape(P, NB * D),
        "src_g": np.ascontiguousarray(padded(src, EP).reshape(NG, TILES, P).transpose(0, 2, 1)),
        "dst_row": dp,
        "dst_tiles": np.ascontiguousarray(dp.reshape(NG * TILES, P).T),
        "ef_t": np.ascontiguousarray(padded(edge_attr_16, EP).T),
        "sh_tiles": np.ascontiguousarray(padded(edge_attr_4, EP).reshape(NG * TILES, P, DEA).transpose(1, 0, 2)).reshape(P, -1),
        "es_t": np.ascontiguousarray(padded(edge_attr_8, EP).T).reshape(P, EC),
        "W1m": np.asarray(L0_gnn_W1m), "b1m": np.asarray(L0_gnn_b1m),
        "W2m_t": np.ascontiguousarray(np.asarray(L0_gnn_W2m).T), "b2m": np.asarray(L0_gnn_b2m),
        "W1u": np.asarray(L0_gnn_W1u), "b1u": np.asarray(L0_gnn_b1u),
        "W2u": np.asarray(L0_gnn_W2u), "b2u": np.asarray(L0_gnn_b2u),
        "fc_w1": np.asarray(L1_gnn_fc_w1), "fc_w2": np.asarray(L1_gnn_fc_w2),
    }
    nc = bacc.Bacc("TRN2", target_bir_lowering=False, num_devices=1)
    ins = {n: nc.dram_tensor(f"in_{n}", a.shape, mybir.dt.from_np(a.dtype), kind="ExternalInput").ap()
           for n, a in arrays.items()}
    out = nc.dram_tensor("out_x", (N, D), F32, kind="ExternalOutput").ap()
    gnn_program(nc, **ins, out=out)
    r = run_bass_kernel_spmd(nc, [{f"in_{n}": a for n, a in arrays.items()}], core_ids=[0])
    return r.results[0]["out_x"]
```

```python
from contextlib import ExitStack

import numpy as np
import concourse.bass as bass
from concourse import mybir

ALU = mybir.AluOpType
ACT = mybir.ActivationFunctionType
AX_X = mybir.AxisListType.X
F32 = mybir.dt.float32
BF16 = mybir.dt.bfloat16
I32 = mybir.dt.int32

P = 128
N, D = 3125, 32
E = 50000
TILES = 4
GE = TILES * P
NG = -(-E // GE)
EP = NG * GE
DEF, DEA, DES = 16, 4, 8
WIN = P - DEF
NO_DST = 1 << 20
OFF_TABLE = 3200
NB = -(-(OFF_TABLE + WIN) // P)
NT = NB * P
HB = NB // 2
DH = 64
HID = 256
MUL = 8
NCH = -(-NT // 512)
SLOTS = 4
LEAD = 2
ROUNDS = (NG - LEAD) // SLOTS
SPLIT = 3
KS = SPLIT * SPLIT * DES
EC = EP // 16
EPS = 1e-5
HSCALE = float(np.sqrt(2.0) / (np.sqrt(DES) * np.sqrt(HID)))
OSCALE = float(1.0 / np.sqrt(E / N))
C_S = float(np.sqrt(1.0 / 128.0)) * HSCALE * OSCALE
C_V = float(np.sqrt(3.0 / 128.0) / np.sqrt(3.0)) * HSCALE * OSCALE
C_S3 = C_S / float(np.sqrt(3.0))

MAX_SWEEPS = -(-N // WIN)

assert LEAD + ROUNDS * SLOTS == NG and N <= OFF_TABLE and NB == 2 * HB


class Group:

    def __init__(self, p, i, c):
        self.p, self.i, self.c = p, i, c
        self.slot = c % SLOTS

    def back(self, n):
        return Group(self.p, self.i, self.c - n)

    @property
    def at(self):
        return self.i * SLOTS + self.c

    def count(self, more):
        return self.p * NG + self.i * SLOTS + (self.c + 1 + more)

    def filled(self, each):
        uses = len(range(self.slot, NG, SLOTS))
        return self.p * (uses * each) + self.i * each + (self.c // SLOTS + 1) * each


def sweep(eng, p, step, drain):
    for c in range(LEAD):
        step(Group(p, 0, c))
    with eng.Fori(0, ROUNDS) as i:
        for c in range(LEAD, LEAD + SLOTS):
            step(Group(p, i, c))
    drain(Group(p, 0, NG))


def gnn_program(nc, x_t, x_rows, src_g, dst_row, dst_tiles, ef_t, sh_tiles, es_t,
                W1m, b1m, W2m_t, b2m, W1u, b1u, W2u, b2u, fc_w1, fc_w2, fold_rows, out):
    with ExitStack() as ctx:
        def sb(name, shape, dt=F32):
            return ctx.enter_context(nc.sbuf_tensor(name, shape, dt))

        def sem(name):
            return ctx.enter_context(nc.semaphore(name))

        def sems(name):
            return [sem(f"{name}{s}") for s in range(SLOTS)]

        src_table = nc.dram_tensor("src_table", [NT, DH], F32).ap()
        dst_table = nc.dram_tensor("dst_table", [NT, DH], F32).ap()
        x1_table = nc.dram_tensor("x1_table", [NT, D], F32).ap()
        es_stack = nc.dram_tensor("es_stack", [KS, EP], BF16).ap()
        range_rows = nc.dram_tensor("range_rows", [NG, 2], I32).ap()

        upd_hid = sb("upd_hid", [DH + 1, NT])
        xt1 = upd_hid
        upd_in = sb("upd_in", [P, NT])
        sums1 = sb("sums1", [P, NT])
        tables = sb("tables", [P, 2, NB, DH])
        x_nm = sb("x_nm", [P, NB, D])
        y = sb("y", [P, NB, D])
        yy = sb("yy", [P, NB, D])
        total = sb("total", [P, NB])
        squares = sb("squares", [P, NB])
        eps = sb("eps", [P, 1])
        std = sb("std", [P, NB])
        rstd = sb("rstd", [P, NB])
        x1 = sb("x1", [P, NB, D])
        out_sb = sb("out_sb", [P, NB, D])
        w_tab = sb("w_tab", [D + 1, 2 * DH])
        w_msg_t = sb("w_msg_t", [D, DH + 1])
        w_upd_a = sb("w_upd_a", [D, DH])
        w_upd = sb("w_upd", [P, DH])
        b_upd = sb("b_upd", [DH, 1])
        w_out = sb("w_out", [DH + 1, D])
        w1s = sb("w1s", [KS, HID], BF16)
        w1f = sb("w1f", [DES, HID])
        w1p = [sb(f"w1p{n}", [DES, HID], BF16) for n in range(SPLIT)]
        w2 = sb("w2", [P, 2, HID])
        fold = sb("fold", [P, D])
        iota_i = sb("iota_i", [P, P], I32)
        iota = sb("iota", [P, P])
        part_i = sb("part_i", [P, 1], I32)
        part = sb("part", [P, 1])
        dst_g = sb("dst_g", [NG, GE], I32)
        dst_in = sb("dst_in", [NG, GE])
        ranges = sb("ranges", [NG, 2], I32)
        range_row = sb("range_row", [1, NG, 2], I32)
        spans = sb("spans", [1, NG])
        span = sb("span", [1, 1])
        windows = sb("windows", [1, 1])
        reached = sb("reached", [1, MAX_SWEEPS])
        sweeps = sb("sweeps", [1, 1], I32)
        range_all = sb("range_all", [P, NG, 2], I32)
        base = sb("base", [P, NG])
        base_at = sb("base_at", [1, NG], I32)
        shift = sb("shift", [P, 1])
        node_of = sb("node_of", [P, NG])
        dst_l = sb("dst_l", [P, NG, TILES], I32)
        rel = sb("rel", [P, NG, TILES])
        neg_rel = sb("neg_rel", [P, NG, TILES])
        es = sb("es", [P, EC])
        esp = [sb(f"esp{n}", [P, EC], BF16) for n in range(SPLIT)]
        sh = sb("sh", [P, NG * TILES, DEA])
        sh8 = sb("sh8", [P, NG * TILES, 2 * DEA])
        src_i = [sb(f"src_i{s}", [P, TILES], I32) for s in range(SLOTS)]
        src_i1 = [sb(f"src_i1{s}", [P, TILES], I32) for s in range(SLOTS)]
        dst_b = [sb(f"dst_b{s}", [P, GE], I32) for s in range(SLOTS)]
        hot_t = [sb(f"hot_t{s}", [P, GE]) for s in range(SLOTS)]
        hot = [sb(f"hot{s}", [P, TILES, WIN]) for s in range(SLOTS)]
        d_win = [sb(f"d_win{s}", [P, DH]) for s in range(SLOTS)]
        gat0 = [sb(f"gat0{s}", [P, TILES, DH]) for s in range(SLOTS)]
        pre = [sb(f"pre{b}", [P, TILES, DH]) for b in range(2)]
        hid = [sb(f"hid{b}", [P, TILES, DH + 1]) for b in range(2)]
        gat1 = [sb(f"gat1{s}", [P, TILES, D]) for s in range(SLOTS)]
        es_in = [sb(f"es_in{s}", [KS, GE], BF16) for s in range(SLOTS)]
        hid1 = [sb(f"hid1{b}", [P, 2, GE]) for b in range(2)]
        away = sb("away", [P, TILES, WIN])
        feat = [sb(f"feat{b}", [P, TILES, 5 * MUL]) for b in range(2)]
        vv = sb("vv", [P, TILES, 3, MUL])
        pa = sb("pa", [P, TILES, 2 * MUL * MUL])
        pv = sb("pv", [P, TILES, 4, MUL * MUL])
        msg = [sb(f"msg{b}", [P, TILES, 2 * D]) for b in range(2)]
        x1_by_i = sb("x1_by_i", [P, NB, D])

        big = [ctx.enter_context(nc.psum_tensor(f"big{n}", [P, 1024], F32)) for n in range(3)]
        small = [ctx.enter_context(nc.psum_tensor(f"small{n}", [P, 512], F32)) for n in range(2)]
        banks = [b[:, 512 * h:512 * h + 512] for b in big for h in range(2)] + [s[:, :] for s in small]
        pre_ps = [big[2][:, 0:TILES * DH], big[2][:, 512:512 + TILES * DH]]
        hid_ps = big[2]
        w_ps = [b[:, :].rearrange("p (t n) -> p t n", t=TILES) for b in big[0:2]]

        x_in, tab_w, upd_w, dst_grouped, dst_by_tile, es_loaded, mlp1_w, sh_loaded = (
            sem(n) for n in ("x_in", "tab_w", "upd_w", "dst_grouped", "dst_by_tile", "es_loaded", "mlp1_w",
                             "sh_loaded"))
        cleared, nodes_in, ef_w, iotas, table_ps, table_act, table_dve = (
            sem(n) for n in ("cleared", "nodes_in", "ef_w", "iotas", "table_ps", "table_act", "table_dve"))
        src_table_out, dst_table_out, ranges_set, ranges_out, range_row_in, range_all_in = (
            sem(n) for n in ("src_table_out", "dst_table_out", "ranges_set", "ranges_out", "range_row_in",
                             "range_all_in"))
        sweeps_set, windows_set, es_cast, es_rest, es_parts_out, w1_parts, w1_stacked = (
            sem(n) for n in ("sweeps_set", "windows_set", "es_cast", "es_rest", "es_parts_out", "w1_parts",
                             "w1_stacked"))
        dve_chain = sem("dve_chain")
        window_base, sh_scaled, hot_away, vec_feats, vec_prods, vec_sums, scaled_feats = (
            sem(n) for n in ("window_base", "sh_scaled", "hot_away", "vec_feats", "vec_prods", "vec_sums",
                             "scaled_feats"))
        shifted = sem("shifted")
        tab_zero, scal_feats, indices_seen = sem("tab_zero"), sem("scal_feats"), sem("indices_seen")
        src_in, dstb_in, pre_in, gathered0, es_landed, gathered1 = (
            sems(n) for n in ("src_in", "dstb_in", "pre_in", "gathered0", "es_landed", "gathered1"))
        src1_in = sems("src1_in")
        hot_ready, pre_mm, pre_sum, relu0, seg0, added0 = (
            sem(n) for n in ("hot_ready", "pre_mm", "pre_sum", "relu0", "seg0", "added0"))
        upd_mm, upd_w_mm, upd_w_set, upd_relu, y_mm, centred, squared, var_set, std_set, x1_set, x1_out = (
            sem(n) for n in ("upd_mm", "upd_w_mm", "upd_w_set", "upd_relu", "y_mm", "centred", "squared", "var_set", "std_set", "x1_set",
                             "x1_out"))
        hid_mm, relu1, w_mm, prods, hot1, msgs, seg1, added1 = (
            sem(n) for n in ("hid_mm", "relu1", "w_mm", "prods", "hot1", "msgs", "seg1", "added1"))
        fold_mm, out_set, out_done = (sem(n) for n in ("fold_mm", "out_set", "out_done"))

        block = ctx.enter_context(nc.Block())

        @block.sync
        def _(sp):
            sp.dma_start(dst_g[:, :], dst_row.rearrange("(g e) -> g e", g=NG)).then_inc(dst_grouped, 16)
            sp.dma_start(xt1[0:D + 1, :], x_t).then_inc(x_in, 16)
            sp.dma_start(dst_l[:, :, :].rearrange("p g t -> p (g t)"), dst_tiles).then_inc(dst_by_tile, 16)
            sp.wait_ge(ranges_set, 2)
            sp.dma_start(range_rows, ranges[:, :]).then_inc(ranges_out, 16)
            sp.wait_ge(ranges_out, 16)
            sp.dma_start(range_row[:, :, :], range_rows.rearrange("(a g) r -> a g r", a=1)).then_inc(range_row_in, 16)
            sp.dma_start(range_all[:, :, :].rearrange("p g r -> p (g r)"),
                         range_rows.rearrange("g r -> (g r)").partition_broadcast(P)).then_inc(range_all_in, 16)
            for d in d_win:
                sp.dma_start(d[WIN:P, :], W1m[2 * D:2 * D + DEF, :]).then_inc(ef_w, 16)
            sp.wait_ge(sweeps_set, 1)
            n_sweeps = sp.value_load(sweeps[0:1, 0:1], min_val=1, max_val=MAX_SWEEPS)

            def load0(g):
                sp.wait_ge(pre_sum, g.count(0))
                sp.dma_start(src_i[g.slot][:, :], src_g[bass.ds(g.at, 1), :, :].rearrange("a p t -> (a p) t")).then_inc(src_in[g.slot], 16)
                sp.dma_start(dst_b[g.slot][:, :],
                             dst_row[bass.ds(g.at * GE, GE)].partition_broadcast(P)).then_inc(dstb_in[g.slot], 16)
                sp.dma_start(hot_t[g.slot][WIN:P, :], ef_t[:, bass.ds(g.at * GE, GE)]).then_inc(pre_in[g.slot], 16)
                first = sp.value_load(base_at[0:1, bass.ds(g.at, 1)], min_val=0, max_val=OFF_TABLE)
                sp.dma_start(d_win[g.slot][0:WIN, :], dst_table[bass.ds(first, WIN), :]).then_inc(pre_in[g.slot], 16)

            sp.wait_ge(dst_table_out, 16)
            with sp.Fori(0, n_sweeps) as p:
                sp.wait_ge(windows_set, p + 1)
                sweep(sp, p, load0, lambda g: None)

            sp.wait_ge(es_parts_out, 16 * SPLIT * SPLIT)

            def load1(g):
                sp.wait_ge(msgs, g.count(0))
                sp.dma_start(src_i1[g.slot][:, :], src_g[bass.ds(g.at, 1), :, :].rearrange("a p t -> (a p) t")).then_inc(src1_in[g.slot], 16)
                sp.dma_start(es_in[g.slot][:, :], es_stack[:, bass.ds(g.at * GE, GE)]).then_inc(es_landed[g.slot], 16)

            with sp.Fori(0, n_sweeps) as p:
                sweep(sp, p, load1, lambda g: None)

            sp.wait_ge(out_set, 1)
            full = N // NB
            sp.dma_start(out[0:full * NB, :].rearrange("(p b) f -> p (b f)", b=NB),
                         out_sb[0:full, :, :].rearrange("p b f -> p (b f)")).then_inc(out_done, 16)
            sp.dma_start(out[full * NB:N, :].rearrange("(a b) f -> a (b f)", a=1),
                         out_sb[full:full + 1, 0:N - full * NB, :].rearrange("p b f -> p (b f)")).then_inc(out_done, 16)
            sp.wait_ge(out_done, 32)

        @block.gpsimd
        def _(pool):
            pool.iota(iota_i[:, :], [[1, P]], base=0, channel_multiplier=0).then_inc(iotas, 1)
            pool.iota(part_i[:, :], [[0, 1]], base=0, channel_multiplier=1).then_inc(iotas, 1)
            pool.wait_ge(iotas, 2)
            for n, (rows, value) in enumerate(((w_upd[DH:P - D, :], 0.0), (upd_in[0:P - D, :], 0.0), (sums1[:, :], 0.0),
                                               (upd_hid[DH:DH + 1, :], 1.0))):
                pool.memset(rows, value).then_inc(cleared, 1)
                pool.wait_ge(cleared, n + 1)
            pool.wait_ge(sweeps_set, 1)
            n_sweeps = pool.value_load(sweeps[0:1, 0:1], min_val=1, max_val=MAX_SWEEPS)
            pool.wait_ge(src_table_out, 16)

            def gather0(g):
                pool.wait_ge(src_in[g.slot], g.filled(16))
                pool.sem_inc(indices_seen, 1)
                for t in range(TILES):
                    pool.indirect_dma_start(
                        out=gat0[g.slot][:, t, :], out_offset=None, in_=src_table,
                        in_offset=bass.IndirectOffsetOnAxis(ap=src_i[g.slot][:, t:t + 1], axis=0),
                    ).then_inc(gathered0[g.slot], 16)

            with pool.Fori(0, n_sweeps) as p:
                sweep(pool, p, gather0, lambda g: None)

            pool.wait_ge(x1_out, 16)

            def gather1(g):
                pool.wait_ge(src1_in[g.slot], g.filled(16))
                pool.sem_inc(indices_seen, 1)
                for t in range(TILES):
                    pool.indirect_dma_start(
                        out=gat1[g.slot][:, t, :], out_offset=None, in_=x1_table,
                        in_offset=bass.IndirectOffsetOnAxis(ap=src_i1[g.slot][:, t:t + 1], axis=0),
                    ).then_inc(gathered1[g.slot], 16)

            with pool.Fori(0, n_sweeps) as p:
                sweep(pool, p, gather1, lambda g: None)

        @block.tensor
        def _(pe):
            pe.wait_ge(x_in, 16)
            pe.wait_ge(tab_w, 48)
            pe.wait_ge(tab_zero, 1)
            xt_by_b = xt1[0:D + 1, :].rearrange("k (p b) -> k b p", b=NB)
            for c in range(NCH):
                for b in range(4 * c, min(4 * c + 4, NB)):
                    k = b - 4 * c
                    mm = pe.matmul(banks[c][:, k * P:(k + 1) * P], xt_by_b[:, b, :], w_tab[:, :],
                                   start=True, stop=True)
                mm.then_inc(table_ps, 1)
            pe.wait_ge(upd_w, 16 * 8)
            pe.matmul(banks[7][0:DH + 1, 0:DH], w_msg_t[:, :], w_upd_a[:, :], start=True, stop=True).then_inc(upd_w_mm, 1)
            pe.wait_ge(sweeps_set, 1)
            n_sweeps = pe.value_load(sweeps[0:1, 0:1], min_val=1, max_val=MAX_SWEEPS)
            pe.wait_ge(table_act, NCH // 2)
            pe.wait_ge(table_dve, NCH - NCH // 2)
            pe.wait_ge(upd_w_set, 1)
            pe.wait_ge(ef_w, 16 * SLOTS)

            def pre_products(g):
                pe.wait_ge(pre_in[g.slot], g.filled(32))
                pe.wait_ge(hot_ready, g.count(0))
                pe.wait_ge(pre_sum, g.count(SLOTS - 2))
                for t in range(TILES):
                    mm = pe.matmul(pre_ps[g.slot % 2][:, t * DH:(t + 1) * DH], hot_t[g.slot][:, t * P:(t + 1) * P],
                                   d_win[g.slot][:, :], start=True, stop=True)
                mm.then_inc(pre_mm, 1)

            def sum0(g):
                pe.wait_ge(relu0, g.count(0))
                pe.wait_ge(added0, g.count(0))
                for t in range(TILES):
                    mm = pe.matmul(small[g.slot % 2][0:DH + 1, 0:WIN], hid[g.slot % 2][:, t, :], hot[g.slot][:, t, :],
                                   start=t == 0, stop=t == TILES - 1)
                mm.then_inc(seg0, 1)

            def step0(g):
                if g.c >= 2:
                    sum0(g.back(2))
                pre_products(g)

            def drain0(g):
                sum0(g.back(2))
                sum0(g.back(1))

            with pe.Fori(0, n_sweeps) as p:
                sweep(pe, p, step0, drain0)

            pe.wait_ge(added0, n_sweeps * NG + 2)
            pe.wait_ge(nodes_in, 32)
            pe.wait_ge(cleared, 4)
            for c in range(NCH):
                w = min(512, NT - 512 * c)
                pe.matmul(banks[c][0:DH, 0:w], w_upd[:, :], upd_in[:, 512 * c:512 * c + w],
                          start=True, stop=True).then_inc(upd_mm, 1)
            pe.wait_ge(upd_relu, NCH)
            hid_by_b = upd_hid[:, :].rearrange("k (p b) -> k b p", b=NB)
            for h in range(2):
                for b in range(HB):
                    mm = pe.matmul(small[h][:, b * D:(b + 1) * D], hid_by_b[:, h * HB + b, :], w_out[:, :],
                                   start=True, stop=True)
                mm.then_inc(y_mm, 1)

            pe.wait_ge(w1_stacked, 16 * SPLIT * SPLIT)
            pe.wait_ge(mlp1_w, 16 * 4)

            def hidden1(g):
                pe.wait_ge(es_landed[g.slot], g.filled(16))
                pe.wait_ge(relu1, g.count(0))
                for c in range(2):
                    mm = pe.matmul(hid_ps[:, c * GE:(c + 1) * GE], w1s[:, c * P:(c + 1) * P], es_in[g.slot][:, :],
                                   start=True, stop=True)
                mm.then_inc(hid_mm, 1)

            def weights1(g):
                pe.wait_ge(relu1, g.count(1))
                pe.wait_ge(prods, g.count(0))
                for t in range(TILES):
                    for c in range(2):
                        mm = pe.matmul(w_ps[g.slot % 2][:, t, :], hid1[g.slot % 2][:, c, t * P:(t + 1) * P],
                                       w2[:, c, :], start=c == 0, stop=c == 1)
                mm.then_inc(w_mm, 1)

            def sum1(g):
                pe.wait_ge(msgs, g.count(SLOTS))
                pe.wait_ge(hot1, g.count(1))
                pe.wait_ge(added1, g.count(0))
                for t in range(TILES):
                    mm = pe.matmul(small[g.slot % 2][t % 2 * 2 * D:(t % 2 + 1) * 2 * D, 0:WIN], msg[g.slot % 2][:, t, :],
                                   hot[g.slot][:, t, :], start=t < 2, stop=t >= 2)
                mm.then_inc(seg1, 1)

            def step1(g):
                hidden1(g)
                if g.c >= 1:
                    weights1(g.back(1))
                if g.c >= 2:
                    sum1(g.back(2))

            def drain1(g):
                weights1(g.back(1))
                sum1(g.back(2))
                sum1(g.back(1))

            with pe.Fori(0, n_sweeps) as p:
                sweep(pe, p, step1, drain1)

            pe.wait_ge(added1, n_sweeps * NG + 2)
            sums_by_b = sums1[:, :].rearrange("k (p b) -> k b p", b=NB)
            for h in range(2):
                for b in range(HB):
                    mm = pe.matmul(banks[h][:, b * D:(b + 1) * D], sums_by_b[:, h * HB + b, :], fold[:, :],
                                   start=True, stop=True)
                mm.then_inc(fold_mm, 1)

        @block.scalar
        def _(act):
            act.dma_start(w_tab[0:D, 0:DH], W1m[0:D, :]).then_inc(tab_w, 16)
            act.dma_start(w_tab[0:D, DH:2 * DH], W1m[D:2 * D, :]).then_inc(tab_w, 16)
            act.dma_start(w_tab[D:D + 1, 0:DH], b1m.rearrange("(a n) -> a n", a=1)).then_inc(tab_w, 16)
            act.dma_start(w_msg_t[:, 0:DH], W2m_t).then_inc(upd_w, 16)
            act.dma_start(w_msg_t[:, DH:DH + 1], b2m.rearrange("(n a) -> n a", a=1)).then_inc(upd_w, 16)
            act.dma_start(w_upd_a[:, :], W1u[D:2 * D, :]).then_inc(upd_w, 16)
            act.dma_start(b_upd[:, :], b1u.rearrange("(n a) -> n a", a=1)).then_inc(upd_w, 16)
            act.dma_start(w_out[0:DH, :], W2u).then_inc(upd_w, 16)
            act.dma_start(w_out[DH:DH + 1, :], b2u.rearrange("(a n) -> a n", a=1)).then_inc(upd_w, 16)
            act.dma_start(w_upd[P - D:P, :], W1u[0:D, :]).then_inc(upd_w, 16)
            for c in range(1, NCH, 2):
                act.wait_ge(table_ps, c + 1)
                nb = min(4, NB - 4 * c)
                act.activation(tables[:, :, 4 * c:4 * c + nb, :],
                               banks[c][:, 0:nb * P].rearrange("p (b h f) -> p h b f", h=2, f=DH),
                               ACT.Copy).then_inc(table_act, 1)
            act.wait_ge(table_act, NCH // 2)
            act.wait_ge(table_dve, NCH - NCH // 2)
            act.dma_start(src_table.rearrange("(p b) f -> p (b f)", b=NB),
                          tables[:, 1, :, :].rearrange("p b f -> p (b f)")).then_inc(src_table_out, 16)
            act.dma_start(dst_table.rearrange("(p b) f -> p (b f)", b=NB),
                          tables[:, 0, :, :].rearrange("p b f -> p (b f)")).then_inc(dst_table_out, 16)
            act.dma_start(es[:, :], es_t).then_inc(es_loaded, 16)
            act.dma_start(sh[:, :, :].rearrange("p t k -> p (t k)"), sh_tiles).then_inc(sh_loaded, 16)
            act.dma_start(upd_in[P - D:P, :], x_t[0:D, :]).then_inc(nodes_in, 16)
            act.dma_start(x_nm[:, :, :].rearrange("p b f -> p (b f)"), x_rows).then_inc(nodes_in, 16)
            act.dma_start(fold[:, :], fold_rows).then_inc(upd_w, 16)
            w2_rows = fc_w2.rearrange("(c p) n -> p c n", c=2)
            act.dma_start(w1f[:, :], fc_w1).then_inc(mlp1_w, 16)
            act.dma_start(w2[:, :, 0:64], w2_rows[:, :, 64:128]).then_inc(mlp1_w, 16)
            act.dma_start(w2[:, :, 64:128], w2_rows[:, :, 0:64]).then_inc(mlp1_w, 16)
            act.dma_start(w2[:, :, 128:256], w2_rows[:, :, 128:256]).then_inc(mlp1_w, 16)
            act.wait_ge(cleared, 4)
            act.wait_ge(upd_w_mm, 1)
            act.activation(w_upd[0:DH + 1, :], banks[7][0:DH + 1, 0:DH], ACT.Copy).then_inc(upd_w_set, 1)
            act.wait_ge(es_loaded, 16)
            for n in range(SPLIT):
                if n:
                    act.wait_ge(es_rest, n)
                act.activation(esp[n][:, :], es[:, :], ACT.Copy).then_inc(es_cast, 1)
            act.wait_ge(es_cast, SPLIT)
            for j in range(SPLIT):
                for i in range(SPLIT):
                    r = (j * SPLIT + i) * DES
                    act.dma_start(es_stack[r:r + DES, :].rearrange("f (c e) -> (f c) e", e=EC),
                                  esp[i][:, :]).then_inc(es_parts_out, 16)
            act.wait_ge(w1_parts, 3)
            for j in range(SPLIT):
                for i in range(SPLIT):
                    r = (j * SPLIT + i) * DES
                    act.dma_start(w1s[r:r + DES, :], w1p[j][:, :]).then_inc(w1_stacked, 16)
            act.wait_ge(sh_loaded, 16)
            act.activation(sh8[:, :, 0:1], sh[:, :, 0:1], ACT.Copy, scale=C_S).then_inc(sh_scaled, 1)
            act.activation(sh8[:, :, 1:DEA], sh[:, :, 1:DEA], ACT.Copy, scale=C_S3).then_inc(sh_scaled, 1)
            act.activation(sh8[:, :, DEA:2 * DEA], sh[:, :, :], ACT.Copy, scale=C_V).then_inc(sh_scaled, 1)
            act.wait_ge(sweeps_set, 1)
            n_sweeps = act.value_load(sweeps[0:1, 0:1], min_val=1, max_val=MAX_SWEEPS)

            def relu_0(g):
                act.wait_ge(pre_sum, g.count(SLOTS))
                act.wait_ge(seg0, g.count(0))
                act.activation(hid[g.slot % 2][:, :, 0:DH], pre[g.slot % 2][:, :, :], ACT.Relu).then_inc(relu0, 1)

            with act.Fori(0, n_sweeps) as p:
                sweep(act, p, relu_0, lambda g: None)

            for c in range(NCH):
                w = min(512, NT - 512 * c)
                act.wait_ge(upd_mm, c + 1)
                act.activation(upd_hid[0:DH, 512 * c:512 * c + w], banks[c][0:DH, 0:w], ACT.Relu,
                               bias=b_upd[:, :]).then_inc(upd_relu, 1)

            def norm_parts(turn):
                for h in range(2):
                    half = slice(h * HB, (h + 1) * HB)
                    act.wait_ge(centred, 2 * turn + h + 1)
                    act.activation(y[:, half, :], yy[:, half, :], ACT.Square).then_inc(squared, 1)
                for h in range(2):
                    half = slice(h * HB, (h + 1) * HB)
                    act.wait_ge(var_set, 2 * turn + h + 1)
                    act.activation(std[:, half], squares[:, half], ACT.Sqrt, scale=1.0 / D,
                                   bias=eps[:, :]).then_inc(std_set, 1)

            norm_parts(0)
            act.wait_ge(x1_set, 1)
            act.dma_start(x1_table.rearrange("(p b) f -> p (b f)", b=NB),
                          x1_by_i[:, :, :].rearrange("p b f -> p (b f)")).then_inc(x1_out, 16)

            def relu_1(g):
                act.wait_ge(hid_mm, g.count(0))
                act.wait_ge(w_mm, g.count(0))
                act.activation(hid1[g.slot % 2][:, :, :].rearrange("p c e -> p (c e)"), hid_ps[:, :],
                               ACT.Relu).then_inc(relu1, 1)

            def hot_1(g):
                act.wait_ge(seg1, g.count(0))
                act.wait_ge(hot1, g.count(0))
                for t in range(TILES):
                    last = act.activation(away[:, t, :], iota[:, 0:WIN], ACT.Square,
                                          bias=neg_rel[:, bass.ds(g.at, 1), t:t + 1].rearrange("p a b -> p (a b)"))
                last.then_inc(hot_away, 1)
                act.wait_ge(hot_away, g.count(0))
                act.activation(hot[g.slot][:, :, :], away[:, :, :], ACT.Relu, scale=-1.0, bias=1.0).then_inc(hot1, 1)

            def scale_1(g):
                act.wait_ge(gathered1[g.slot], g.filled(16 * TILES))
                act.wait_ge(prods, g.count(0))
                for t in range(TILES):
                    last = act.activation(feat[g.slot % 2][:, t, MUL:5 * MUL], gat1[g.slot][:, t, :], ACT.Copy,
                                          scale=sh8[:, bass.ds(g.at * TILES + t, 1), 0:1].rearrange("p a b -> p (a b)"))
                last.then_inc(scaled_feats, 1)

            def step1(g):
                relu_1(g)
                hot_1(g)
                scale_1(g)

            with act.Fori(0, n_sweeps) as p:
                act.wait_ge(windows_set, n_sweeps + p + 2)
                sweep(act, p, step1, lambda g: None)

            norm_parts(1)

        @block.vector
        def _(dve):
            done = [0]

            def link(ins):
                done[0] += 1
                ins.then_inc(dve_chain, 1)
                dve.wait_ge(dve_chain, done[0])

            link(dve.memset(w_tab[D:D + 1, DH:2 * DH], 0.0))
            dve.memset(shift[:, :], 0.0)
            dve.memset(eps[:, :], EPS).then_inc(tab_zero, 1)
            dve.wait_ge(dst_grouped, 16)
            dve.tensor_reduce(ranges[:, 0:1], dst_g[:, :], AX_X, ALU.min).then_inc(ranges_set, 1)
            link(dve.scalar_tensor_tensor(out=dst_in[:, :], in0=dst_g[:, :], scalar=float(NO_DST), in1=dst_g[:, :],
                                          op0=ALU.is_lt, op1=ALU.mult))
            dve.tensor_reduce(ranges[:, 1:2], dst_in[:, :], AX_X, ALU.max).then_inc(ranges_set, 1)
            dve.wait_ge(iotas, 2)
            dve.tensor_copy(iota[:, :], iota_i[:, :])
            link(dve.tensor_copy(part[:, :], part_i[:, :]))

            def evacuate(c):
                dve.wait_ge(table_ps, c + 1)
                nb = min(4, NB - 4 * c)
                dve.tensor_copy(tables[:, :, 4 * c:4 * c + nb, :],
                                banks[c][:, 0:nb * P].rearrange("p (b h f) -> p h b f", h=2, f=DH)).then_inc(table_dve, 1)

            for c in range(0, NCH, 2):
                evacuate(c)
            dve.wait_ge(range_row_in, 16)
            link(dve.tensor_tensor(spans[:, :], range_row[:, :, 1], range_row[:, :, 0], ALU.subtract))
            link(dve.tensor_reduce(span[:, :], spans[:, :], AX_X, ALU.max))
            link(dve.tensor_scalar(reached[:, :], iota[0:1, 0:MAX_SWEEPS], float(WIN), span[:, 0:1], ALU.mult, ALU.is_le))
            link(dve.tensor_reduce(windows[:, :], reached[:, :], AX_X, ALU.add))
            dve.tensor_copy(sweeps[:, :], windows[:, :]).then_inc(sweeps_set, 1)
            dve.wait_ge(range_all_in, 16)
            dve.wait_ge(dst_by_tile, 16)

            def set_windows(sweep_no):
                if not isinstance(sweep_no, int):
                    dve.wait_ge(shifted, sweep_no)
                dve.tensor_scalar(base[:, :], range_all[:, :, 0], shift[:, 0:1], None, ALU.add).then_inc(window_base, 1)
                dve.wait_ge(window_base, sweep_no + 1)
                dve.tensor_scalar(node_of[:, :], base[:, :], part[:, 0:1], None, ALU.add)
                dve.tensor_scalar(base_at[:, :], base[0:1, :], float(OFF_TABLE), None, ALU.min)
                first = base[:, :, None].to_broadcast([P, NG, TILES])
                dve.tensor_tensor(rel[:, :, :], dst_l[:, :, :], first, ALU.subtract)
                dve.tensor_tensor(neg_rel[:, :, :], first, dst_l[:, :, :], ALU.subtract).then_inc(windows_set, 1)
                dve.wait_ge(windows_set, sweep_no + 1)
                dve.tensor_scalar(shift[:, :], shift[:, :], float(WIN), None, ALU.add).then_inc(shifted, 1)

            set_windows(0)
            for s, n in ((pre_sum, SLOTS), (added0, 2), (seg0, 2), (relu1, 1), (prods, 2), (msgs, SLOTS),
                         (added1, 2), (w_mm, 2), (seg1, SLOTS), (hot1, 1)):
                dve.sem_inc(s, n)
            link(dve.memset(hid[0][:, :, :], 1.0))
            link(dve.memset(hid[1][:, :, :], 1.0))
            for n in range(SPLIT - 1):
                dve.wait_ge(es_cast, n + 1)
                dve.tensor_tensor(es[:, :], es[:, :], esp[n][:, :], ALU.subtract).then_inc(es_rest, 1)
            dve.wait_ge(mlp1_w, 16 * 4)
            for n in range(SPLIT):
                dve.tensor_copy(w1p[n][:, :], w1f[:, :]).then_inc(w1_parts, 1)
                if n < SPLIT - 1:
                    dve.wait_ge(w1_parts, n + 1)
                    link(dve.tensor_tensor(w1f[:, :], w1f[:, :], w1p[n][:, :], ALU.subtract))
            n_sweeps = dve.value_load(sweeps[0:1, 0:1], min_val=1, max_val=MAX_SWEEPS)

            def one_hots(g):
                dve.wait_ge(dstb_in[g.slot], g.filled(16))
                dve.tensor_scalar(hot_t[g.slot][0:WIN, :], dst_b[g.slot][0:WIN, :], node_of[0:WIN, bass.ds(g.at, 1)], None,
                                  ALU.is_equal)
                for t in range(TILES):
                    last = dve.tensor_scalar(hot[g.slot][:, t, :], iota[:, 0:WIN],
                                             rel[:, bass.ds(g.at, 1), t:t + 1].rearrange("p a b -> p (a b)"), None,
                                             ALU.is_equal)
                last.then_inc(hot_ready, 1)

            def sum_pre(g):
                dve.wait_ge(gathered0[g.slot], g.filled(16 * TILES))
                dve.wait_ge(pre_mm, g.count(0))
                dve.tensor_tensor(pre[g.slot % 2][:, :, :].rearrange("p t f -> p (t f)"), pre_ps[g.slot % 2],
                                  gat0[g.slot][:, :, :].rearrange("p t f -> p (t f)"), ALU.add).then_inc(pre_sum, 1)

            def add_to_nodes(g, first, acc, rows, summed, credit, added):
                dve.wait_ge(summed, g.count(credit))
                dve.wait_ge(added, g.count(1))
                there = acc[0:rows, bass.ds(first, WIN)]
                dve.tensor_tensor(there, there, small[g.slot % 2][0:rows, 0:WIN], ALU.add).then_inc(added, 1)

            def add0(g):
                first = dve.value_load(base_at[0:1, bass.ds(g.at, 1)], min_val=0, max_val=OFF_TABLE)
                add_to_nodes(g, first, upd_in, DH + 1, seg0, 2, added0)

            def step0(g):
                one_hots(g)
                if g.c >= 2:
                    add0(g.back(2))
                if g.c >= 1:
                    sum_pre(g.back(1))

            def drain0(g):
                add0(g.back(2))
                sum_pre(g.back(1))
                add0(g.back(1))

            def next0(g):
                drain0(g)
                set_windows(g.p + 1)

            with dve.Fori(0, n_sweeps) as p:
                sweep(dve, p, step0, next0)

            def layernorm(src, src_ready, res, turn, normed):
                halves = [slice(h * HB, (h + 1) * HB) for h in range(2)]
                steps = []
                for h, half in enumerate(halves):
                    dve.wait_ge(src_ready, h + 1)
                    steps.append(dve.tensor_tensor(y[:, half, :], src[h][:, 0:HB * D].rearrange("p (b f) -> p b f", f=D),
                                                   res[:, half, :], ALU.add))
                    link(steps[-1])
                    link(dve.tensor_reduce(total[:, half], y[:, half, :], AX_X, ALU.add))
                    dve.scalar_tensor_tensor(out=yy[:, half, :], in0=total[:, half, None].to_broadcast([P, HB, D]),
                                             scalar=-1.0 / D, in1=y[:, half, :], op0=ALU.mult,
                                             op1=ALU.add).then_inc(centred, 1)
                for h, half in enumerate(halves):
                    dve.wait_ge(squared, 2 * turn + h + 1)
                    dve.tensor_reduce(squares[:, half], y[:, half, :], AX_X, ALU.add).then_inc(var_set, 1)
                for h, half in enumerate(halves):
                    dve.wait_ge(std_set, 2 * turn + h + 1)
                    link(dve.reciprocal(rstd[:, half], std[:, half]))
                    last = normed(half, rstd[:, half])
                return last

            def to_x1_by_i(half, r):
                dve.tensor_tensor(x1_by_i[:, half, 0:MUL], yy[:, half, 0:MUL], r[:, :, None].to_broadcast([P, HB, MUL]),
                                  ALU.mult)
                return dve.tensor_tensor(x1_by_i[:, half, MUL:D].rearrange("p b (i u) -> p b u i", i=3),
                                         yy[:, half, MUL:D].rearrange("p b (u i) -> p b u i", i=3),
                                         r[:, :, None, None].to_broadcast([P, HB, MUL, 3]), ALU.mult)

            layernorm(small, y_mm, x_nm, 0, to_x1_by_i).then_inc(x1_set, 1)
            dve.tensor_tensor(x1[:, :, :], yy[:, :, :], rstd[:, :, None].to_broadcast([P, NB, D]), ALU.mult)
            link(dve.memset(shift[:, :], 0.0))
            set_windows(n_sweeps + 1)
            dve.wait_ge(sh_scaled, 3)

            def times_v2(g):
                dve.wait_ge(vec_sums, g.count(0))
                m = msg[g.slot % 2]
                h = sh8[:, bass.ds(g.at * TILES, TILES), DEA + 1:2 * DEA]
                dve.tensor_tensor(m[:, :, 5 * MUL:8 * MUL].rearrange("p t (i w) -> p t i w", i=3),
                                  m[:, :, None, MUL:2 * MUL].to_broadcast([P, TILES, 3, MUL]),
                                  h[:, :, :, None].to_broadcast([P, TILES, 3, MUL]), ALU.mult).then_inc(msgs, 1)

            def step1(g):
                f, m, w, rows = feat[g.slot % 2], msg[g.slot % 2], w_ps[g.slot % 2], gat1[g.slot]
                v2 = sh8[:, bass.ds(g.at * TILES, TILES), 1:DEA]
                if g.c >= 2:
                    first = dve.value_load(base_at[0:1, bass.ds(g.back(2).at, 1)], min_val=0, max_val=OFF_TABLE)
                dve.wait_ge(gathered1[g.slot], g.filled(16 * TILES))
                dve.tensor_tensor(vv[:, :, :, :], rows[:, :, MUL:D].rearrange("p t (i u) -> p t i u", i=3),
                                  v2[:, :, :, None].to_broadcast([P, TILES, 3, MUL]), ALU.mult).then_inc(vec_feats, 1)
                if g.c >= 1:
                    times_v2(g.back(1))
                dve.wait_ge(vec_feats, g.count(0))
                dve.tensor_reduce(f[:, :, 0:MUL], vv[:, :, :, :].rearrange("p t i u -> p t u i"), AX_X,
                                  ALU.add).then_inc(scal_feats, 1)
                dve.wait_ge(w_mm, g.count(2))
                dve.tensor_tensor(pv[:, :, 0, :].rearrange("p t (u w) -> p t u w", w=MUL),
                                  w[:, :, 128:192].rearrange("p t (u w) -> p t u w", w=MUL),
                                  rows[:, :, 0:MUL, None].to_broadcast([P, TILES, MUL, MUL]), ALU.mult)
                dve.wait_ge(scaled_feats, g.count(0))
                dve.tensor_tensor(pv[:, :, 1:4, :].rearrange("p t i (u w) -> p t i u w", w=MUL),
                                  w[:, :, None, 192:256].rearrange("p t i (u w) -> p t i u w", w=MUL)
                                  .to_broadcast([P, TILES, 3, MUL, MUL]),
                                  f[:, :, 2 * MUL:5 * MUL].rearrange("p t (i u) -> p t i u", i=3)[:, :, :, :, None]
                                  .to_broadcast([P, TILES, 3, MUL, MUL]), ALU.mult).then_inc(vec_prods, 1)
                dve.wait_ge(scal_feats, g.count(0))
                dve.tensor_tensor(pa[:, :, :].rearrange("p t (u w) -> p t u w", w=MUL),
                                  w[:, :, 0:128].rearrange("p t (u w) -> p t u w", w=MUL),
                                  f[:, :, 0:2 * MUL, None].to_broadcast([P, TILES, 2 * MUL, MUL]), ALU.mult).then_inc(prods, 1)
                if g.c >= 2:
                    add_to_nodes(g.back(2), first, sums1, P, seg1, SLOTS, added1)
                dve.wait_ge(vec_prods, g.count(0))
                dve.tensor_reduce(m[:, :, MUL:5 * MUL].rearrange("p t (j w) -> p t j w", w=MUL),
                                  pv[:, :, :, :].rearrange("p t j (u w) -> p t j w u", w=MUL), AX_X,
                                  ALU.add).then_inc(vec_sums, 1)
                dve.wait_ge(prods, g.count(2))
                dve.tensor_reduce(m[:, :, 0:MUL], pa[:, :, :].rearrange("p t (u w) -> p t w u", w=MUL), AX_X, ALU.add)

            def drain1(g):
                times_v2(g.back(1))
                for n in (2, 1):
                    first = dve.value_load(base_at[0:1, bass.ds(g.back(n).at, 1)], min_val=0, max_val=OFF_TABLE)
                    add_to_nodes(g.back(n), first, sums1, P, seg1, SLOTS, added1)
                set_windows(n_sweeps + g.p + 2)

            with dve.Fori(0, n_sweeps) as p:
                sweep(dve, p, step1, drain1)

            def to_out(half, r):
                return dve.tensor_tensor(out_sb[:, half, :], yy[:, half, :], r[:, :, None].to_broadcast([P, HB, D]), ALU.mult)

            layernorm(banks, fold_mm, x1, 1, to_out).then_inc(out_set, 1)


def kernel(x, src, dst, edge_attr_16, edge_attr_4, edge_attr_8, L0_gnn_W1m, L0_gnn_b1m, L0_gnn_W2m, L0_gnn_b2m,
           L0_gnn_W1u, L0_gnn_b1u, L0_gnn_W2u, L0_gnn_b2u, L1_gnn_fc_w1, L1_gnn_fc_w2):
    import concourse.bacc as bacc
    from concourse.bass_utils import run_bass_kernel_spmd

    def padded(a, rows, fill=0):
        a = np.asarray(a)
        full = np.full((rows,) + a.shape[1:], fill, a.dtype)
        full[:a.shape[0]] = a
        return full

    xp = padded(x, NT)
    dp = padded(dst, EP, NO_DST)
    fold = np.zeros((2, 2 * D, D), np.float32)
    for w in range(MUL):
        fold[:, w, w] = 1
        for i in range(3):
            fold[:, [(2 + i) * MUL + w, (5 + i) * MUL + w], MUL + 3 * w + i] = 1
    arrays = {
        "x_t": np.concatenate([xp.T, np.ones((1, NT), xp.dtype)]),
        "x_rows": xp.reshape(P, NB * D),
        "src_g": np.ascontiguousarray(padded(src, EP).reshape(NG, TILES, P).transpose(0, 2, 1)),
        "dst_row": dp,
        "dst_tiles": np.ascontiguousarray(dp.reshape(NG * TILES, P).T),
        "ef_t": np.ascontiguousarray(padded(edge_attr_16, EP).T),
        "sh_tiles": np.ascontiguousarray(padded(edge_attr_4, EP).reshape(NG * TILES, P, DEA).transpose(1, 0, 2)).reshape(P, -1),
        "es_t": np.ascontiguousarray(padded(edge_attr_8, EP).T).reshape(P, EC),
        "W1m": np.asarray(L0_gnn_W1m), "b1m": np.asarray(L0_gnn_b1m),
        "W2m_t": np.ascontiguousarray(np.asarray(L0_gnn_W2m).T), "b2m": np.asarray(L0_gnn_b2m),
        "W1u": np.asarray(L0_gnn_W1u), "b1u": np.asarray(L0_gnn_b1u),
        "W2u": np.asarray(L0_gnn_W2u), "b2u": np.asarray(L0_gnn_b2u),
        "fc_w1": np.asarray(L1_gnn_fc_w1), "fc_w2": np.asarray(L1_gnn_fc_w2),
        "fold_rows": fold.reshape(P, D),
    }
    nc = bacc.Bacc("TRN2", target_bir_lowering=False, num_devices=1)
    ins = {n: nc.dram_tensor(f"in_{n}", a.shape, mybir.dt.from_np(a.dtype), kind="ExternalInput").ap()
           for n, a in arrays.items()}
    out = nc.dram_tensor("out_x", (N, D), F32, kind="ExternalOutput").ap()
    gnn_program(nc, **ins, out=out)
    r = run_bass_kernel_spmd(nc, [{f"in_{n}": a for n, a in arrays.items()}], core_ids=[0])
    return r.results[0]["out_x"]
```

```python
from contextlib import ExitStack

import numpy as np
import concourse.bass as bass
from concourse import mybir

ALU = mybir.AluOpType
ACT = mybir.ActivationFunctionType
AX_X = mybir.AxisListType.X
F32 = mybir.dt.float32
BF16 = mybir.dt.bfloat16
I32 = mybir.dt.int32
I16 = mybir.dt.int16

P = 128
N, D = 3125, 32
E = 50000
TILES = 4
GE = TILES * P
NG = -(-E // GE)
EP = NG * GE
DEF, DEA, DES = 16, 4, 8
WIN = 80
KW = WIN + DEF
NO_DST = 1 << 20
OFF_TABLE = 3200
NB = -(-(OFF_TABLE + WIN) // P)
NT = NB * P
HB = NB // 2
DH = 64
HID = 256
MUL = 8
QUADS = P // D
QP = P // QUADS
HALF = HB * QP
NCH = NT // 2 // HALF
SLOTS = 4
LEAD = 2
ROUNDS = (NG - LEAD) // SLOTS
SPLIT = 3
KS = SPLIT * SPLIT * DES
EC = EP // 16
EPS = 1e-5
HSCALE = float(np.sqrt(2.0) / (np.sqrt(DES) * np.sqrt(HID)))
OSCALE = float(1.0 / np.sqrt(E / N))
C_S = float(np.sqrt(1.0 / 128.0)) * HSCALE * OSCALE
C_V = float(np.sqrt(3.0 / 128.0) / np.sqrt(3.0)) * HSCALE * OSCALE
C_S3 = C_S / float(np.sqrt(3.0))

MAX_SWEEPS = -(-N // WIN)
PICKER = LEAD + 2
STEPS = SLOTS - 1

assert LEAD + ROUNDS * SLOTS == NG and LEAD == NG % SLOTS == 2 and N <= OFF_TABLE and NB == 2 * HB


class Group:

    def __init__(self, p, i, c):
        self.p, self.i, self.c = p, i, c
        self.slot = c % SLOTS

    def back(self, n):
        return Group(self.p, self.i, self.c - n)

    @property
    def at(self):
        return self.i * SLOTS + self.c

    def count(self, more):
        return self.p * NG + self.i * SLOTS + (self.c + 1 + more)

    def slot_used(self):
        return self.count(SLOTS - NG % SLOTS if self.c < NG % SLOTS else 0)

    def filled(self, each):
        uses = len(range(self.slot, NG, SLOTS))
        return self.p * (uses * each) + self.i * each + (self.c // SLOTS + 1) * each

    @property
    def picks(self):
        return self.c == PICKER

    @property
    def prepares(self):
        ends = isinstance(self.i, int) and self.i == ROUNDS - 1 and self.c >= SLOTS
        return self.slot < STEPS and not ends

    @property
    def set(self):
        return self.i + self.c // SLOTS

    def piece(self, more):
        return self.p * ROUNDS * STEPS + self.set * STEPS + (self.slot + 1 + more)

    def sets(self, more):
        return self.p * ROUNDS + self.i + (self.c // SLOTS + more)

    def filled_unpicked(self, each):
        assert not self.picks
        return self.filled(each) if self.slot != PICKER % SLOTS else (self.p + 1) * each


def sweep(eng, p, step, drain):
    for c in range(LEAD):
        step(Group(p, 0, c))
    with eng.Fori(0, ROUNDS - 1) as i:
        for c in range(LEAD, LEAD + SLOTS):
            step(Group(p, i, c))
    for c in range(LEAD, LEAD + SLOTS):
        step(Group(p, ROUNDS - 1, c))
    drain(Group(p, 0, NG))


def gnn_program(nc, x_t, x_rows, src_g, src_row, dst_row, dst_tiles, ef_t, sh_tiles, es_t,
                W1m, W1m_src_by_i, b1m, W2m_t, b2m, W1u, b1u, W2u, b2u, fc_w1, fc_w2, fold_rows, out):
    with ExitStack() as ctx:
        def sb(name, shape, dt=F32):
            return ctx.enter_context(nc.sbuf_tensor(name, shape, dt))

        def sem(name):
            return ctx.enter_context(nc.semaphore(name))

        def sems(name):
            return [sem(f"{name}{s}") for s in range(SLOTS)]

        src_table = nc.dram_tensor("src_table", [NT, DH], F32).ap()
        dst_table = nc.dram_tensor("dst_table", [NT, DH], F32).ap()
        x1_table = nc.dram_tensor("x1_table", [NT, D], F32).ap()
        es_parts = nc.dram_tensor("es_parts", [SPLIT * DES, EP], BF16).ap()
        range_rows = nc.dram_tensor("range_rows", [NG, 2], I32).ap()

        upd_hid = sb("upd_hid", [P, NT // 2])
        pick = sb("pick", [P, NB, GE], BF16)
        xt1 = pick[0:D + 1, :, :].rearrange("p b e -> p (b e)")[:, 0:2 * NT].bitcast(F32)
        upd_in = sb("upd_in", [P, NT])
        sums1 = sb("sums1", [P, NT])
        tables = sb("tables", [P, 2, NB, DH])
        x_nm = sb("x_nm", [P, NB, D])
        y = tables[:, 0, 0:NB // 2, :].rearrange("p b (h f) -> p (b h) f", f=D)
        x_cen = tables[:, 0, NB // 2:NB, :].rearrange("p b (h f) -> p (b h) f", f=D)
        yy = sb("yy", [P, NB, D])
        total = sb("total", [P, NB])
        squares = sb("squares", [P, NB])
        eps = sb("eps", [P, 1])
        std = sb("std", [P, NB])
        rstd = sb("rstd", [P, NB])
        x1 = sb("x1", [P, NB, D])
        out_sb = x_nm
        w_tab = sb("w_tab", [D + 1, 2 * DH])
        w_msg_t = sb("w_msg_t", [D, DH + 1])
        w_upd_a = sb("w_upd_a", [D, DH])
        w_upd = sb("w_upd", [P, DH])
        b_upd = sb("b_upd", [P, 1])
        w_out = sb("w_out", [P, D])
        w_mean = sb("w_mean", [P, 1])
        b_out = sb("b_out", [P, D])
        w1s = sb("w1s", [KS, HID], BF16)
        w1f = sb("w1f", [DES, HID])
        w1p = [sb(f"w1p{n}", [DES, HID], BF16) for n in range(SPLIT)]
        w2 = sb("w2", [P, 2, HID])
        fold = sb("fold", [P, D])
        iota_i = sb("iota_i", [P, P], I32)
        iota = sb("iota", [P, P])
        part_i = sb("part_i", [P, 1], I32)
        part = sb("part", [P, 1])
        part_node = sb("part_node", [P, 1])
        dst_g = sb("dst_g", [NG, GE], I32)
        dst_in = sb("dst_in", [NG, GE])
        ranges = sb("ranges", [NG, 2], I32)
        range_row = sb("range_row", [1, NG, 2], I32)
        spans = sb("spans", [1, NG])
        span = sb("span", [1, 1])
        windows = sb("windows", [1, 1])
        reached = sb("reached", [1, MAX_SWEEPS])
        sweeps = sb("sweeps", [1, 1], I32)
        range_all = sb("range_all", [P, NG, 2], I32)
        base = sb("base", [P, NG])
        base_at = sb("base_at", [1, NG], I32)
        shift = sb("shift", [P, 1])
        node_of = sb("node_of", [P, NG])
        dst_l = sb("dst_l", [P, NG, TILES], I32)
        neg_rel = sb("neg_rel", [P, NG, TILES])
        es = sb("es", [P, EC])
        esp = [sb(f"esp{n}", [P, EC], BF16) for n in range(SPLIT)]
        sh = sb("sh", [P, NG * TILES, DEA])
        sh8 = sb("sh8", [P, NG * TILES, 2 * DEA])
        src_i = [sb(f"src_i{s}", [P, TILES], I32) for s in range(SLOTS)]
        src_i1 = [sb(f"src_i1{s}", [P, TILES], I32) for s in range(SLOTS)]
        dst_b = [sb(f"dst_b{s}", [P, GE], I32) for s in range(SLOTS)]
        hot_t = [sb(f"hot_t{s}", [KW, GE]) for s in range(SLOTS)]
        hot = [sb(f"hot{s}", [P, TILES, WIN]) for s in range(SLOTS)]
        d_win = [sb(f"d_win{s}", [KW, DH]) for s in range(SLOTS)]
        gat0 = [sb(f"gat0{s}", [P, TILES, DH]) for s in range(SLOTS)]
        pre = [sb(f"pre{b}", [P, TILES, DH]) for b in range(2)]
        hid = [sb(f"hid{b}", [P, TILES, DH + 1]) for b in range(2)]
        gat1 = [sb(f"gat1{s}", [P, TILES, D]) for s in range(SLOTS)]
        es_in = [sb(f"es_in{s}", [KS, GE], BF16) for s in range(SLOTS)]
        hid1_both = sb("hid1_both", [P, 2, 2, GE])
        hid1 = [hid1_both[:, b] for b in range(2)]
        x_parts = (hid1_both[:, :, :, :].rearrange("p b c e -> p (b c e)")[:, 0:NB * SPLIT * D // 2].bitcast(BF16)
                   .rearrange("p (b s f) -> p b s f", s=SPLIT, f=D))
        away = sb("away", [P, TILES, WIN])
        feat = [sb(f"feat{b}", [P, TILES, 6 * MUL]) for b in range(2)]
        vv = sb("vv", [P, TILES, 3, MUL])
        terms = es[:, 0:TILES * 6 * MUL * MUL].rearrange("p (t j n) -> p t j n", t=TILES, j=6)
        msg = [sb(f"msg{b}", [P, TILES, 9 * MUL]) for b in range(2)]

        x_rest = yy
        src_b = sb("src_b", [P, GE], I32)
        src_rel = sb("src_rel", [P, GE], I16)
        picked_t = sb("picked_t", [P, GE])
        w_src = sb("w_src", [P, DH])

        big = [ctx.enter_context(nc.psum_tensor(f"big{n}", [P, 1024], F32)) for n in range(3)]
        small = [ctx.enter_context(nc.psum_tensor(f"small{n}", [P, 512], F32)) for n in range(2)]
        banks = [b[:, 512 * h:512 * h + 512] for b in big for h in range(2)] + [s[:, :] for s in small]
        pre_ps = [big[2][:, 0:TILES * DH], big[2][:, 512:512 + TILES * DH]]
        hid_ps = big[2]
        w_ps = [b[:, :].rearrange("p (t n) -> p t n", t=TILES) for b in big[0:2]]

        x_in, tab_w, upd_w, dst_grouped, dst_by_tile, es_loaded, mlp1_w, sh_loaded = (
            sem(n) for n in ("x_in", "tab_w", "upd_w", "dst_grouped", "dst_by_tile", "es_loaded", "mlp1_w",
                             "sh_loaded"))
        cleared, nodes_in, ef_w, iotas, table_ps, table_dve = (
            sem(n) for n in ("cleared", "nodes_in", "ef_w", "iotas", "table_ps", "table_dve"))
        src_table_out, dst_table_out, ranges_set, ranges_out, range_row_in, range_all_in = (
            sem(n) for n in ("src_table_out", "dst_table_out", "ranges_set", "ranges_out", "range_row_in",
                             "range_all_in"))
        sweeps_set, windows_set, es_cast, es_rest, es_parts_out, w1_parts, w1_stacked = (
            sem(n) for n in ("sweeps_set", "windows_set", "es_cast", "es_rest", "es_parts_out", "w1_parts",
                             "w1_stacked"))
        dve_chain = sem("dve_chain")
        window_base, sh_scaled, hot_away, hot_away0, hot0, vec_feats, vec_sums, scaled_feats = (
            sem(n) for n in ("window_base", "sh_scaled", "hot_away", "hot_away0", "hot0", "vec_feats", "vec_sums",
                             "scaled_feats"))
        shifted = sem("shifted")
        tab_zero, scal_feats, indices_seen, w_out_set, w1_in, std_warm = (
            sem(n) for n in ("tab_zero", "scal_feats", "indices_seen", "w_out_set", "w1_in", "std_warm"))
        src_in, dstb_in, pre_in, gathered0, es_landed, gathered1 = (
            sems(n) for n in ("src_in", "dstb_in", "pre_in", "gathered0", "es_landed", "gathered1"))
        src1_in = sems("src1_in")
        hot_ready, pre_mm, pre_sum, relu0, seg0, added0 = (
            sem(n) for n in ("hot_ready", "pre_mm", "pre_sum", "relu0", "seg0", "added0"))
        upd_mm, upd_w_mm, upd_w_set, upd_relu, y_mm, centred, squared, var_set, std_set, x1_set, x1_out = (
            sem(n) for n in ("upd_mm", "upd_w_mm", "upd_w_set", "upd_relu", "y_mm", "centred", "squared", "var_set",
                             "std_set", "x1_set", "x1_out"))
        hid_mm, relu1, w_mm, prods, hot1, msgs, seg1, added1 = (
            sem(n) for n in ("hid_mm", "relu1", "w_mm", "prods", "hot1", "msgs", "seg1", "added1"))
        srcb_in, pick_ready, pick_used, slot_seen, picked_set, w_src_in, x_in_nm, x_cast, x_left, rel_set = (
            sem(n) for n in ("srcb_in", "pick_ready", "pick_used", "slot_seen", "picked_set", "w_src_in", "x_in_nm",
                             "x_cast", "x_left", "rel_set"))
        fold_mm, out_set, out_done = (sem(n) for n in ("fold_mm", "out_set", "out_done"))

        table_parts = [(h, f) for t in (1, 0) for h in range(2) for f in (2 * t, 2 * t + 1)]

        es_chunks = [slice(k * EC // 4, (k + 1) * EC // 4) for k in range(4)]

        step_blocks = [range(k * NB // STEPS, (k + 1) * NB // STEPS) for k in range(STEPS)]

        block = ctx.enter_context(nc.Block())

        @block.sync
        def _(sp):
            sp.dma_start(xt1[:, :], x_t).then_inc(x_in, 16)
            sp.dma_start(dst_g[:, :], dst_row.rearrange("(g e) -> g e", g=NG)).then_inc(dst_grouped, 16)
            sp.dma_start(dst_l[:, :, :].rearrange("p g t -> p (g t)"), dst_tiles).then_inc(dst_by_tile, 16)
            sp.wait_ge(ranges_set, 2)
            sp.dma_start(range_rows, ranges[:, :]).then_inc(ranges_out, 16)
            sp.wait_ge(ranges_out, 16)
            sp.dma_start(range_row[:, :, :], range_rows.rearrange("(a g) r -> a g r", a=1)).then_inc(range_row_in, 16)
            sp.dma_start(range_all[:, :, :].rearrange("p g r -> p (g r)"),
                         range_rows.rearrange("g r -> (g r)").partition_broadcast(P)).then_inc(range_all_in, 16)
            sp.wait_ge(table_dve, 4)
            sp.dma_start(src_table.rearrange("(p b) f -> p (b f)", b=NB),
                         tables[:, 1, :, :].rearrange("p b f -> p (b f)")).then_inc(src_table_out, 16)
            sp.wait_ge(sweeps_set, 1)
            n_sweeps = sp.value_load(sweeps[0:1, 0:1], min_val=1, max_val=MAX_SWEEPS)

            def load_edges0(g):
                sp.wait_ge(pre_sum, g.slot_used())
                sp.sem_inc(slot_seen, 1)
                if not g.picks:
                    sp.dma_start(src_i[g.slot][:, :],
                                 src_g[bass.ds(g.at, 1), :, :].rearrange("a p t -> (a p) t")).then_inc(src_in[g.slot], 16)
                sp.dma_start(dst_b[g.slot][:, :],
                             dst_row[bass.ds(g.at * GE, GE)].partition_broadcast(P)).then_inc(dstb_in[g.slot], 16)
                sp.dma_start(hot_t[g.slot][WIN:KW, :], ef_t[:, bass.ds(g.at * GE, GE)]).then_inc(pre_in[g.slot], 16)

            def load_window(g):
                if g.c == 0:
                    sp.wait_ge(dst_table_out, 16)
                    sp.wait_ge(windows_set, g.p + 1)
                    sp.sem_inc(slot_seen, 1)
                first = sp.value_load(base_at[0:1, bass.ds(g.at, 1)], min_val=0, max_val=OFF_TABLE)
                sp.dma_start(d_win[g.slot][0:WIN, :], dst_table[bass.ds(first, WIN), :]).then_inc(pre_in[g.slot], 16)

            def load0(g):
                load_edges0(g)
                if g.c >= 1:
                    load_window(g.back(1))
                if g.slot == 0 and g.prepares:
                    sp.wait_ge(rel_set, g.sets(1))
                    sp.sem_inc(slot_seen, 1)
                    first = (g.at + SLOTS) * GE
                    sp.dma_start(src_b[:, :], src_row[bass.ds(first, GE)].partition_broadcast(P)).then_inc(srcb_in, 16)

            with sp.Fori(0, n_sweeps) as p:
                sweep(sp, p, load0, lambda g: load_window(g.back(1)))

            sp.dma_start(fold[:, :], fold_rows).then_inc(nodes_in, 16)
            w2_rows = fc_w2.rearrange("(c p) n -> p c n", c=2)
            for k, n in enumerate((2, 1, 0, 3)):
                sp.dma_start(w2[:, :, k * DH:(k + 1) * DH], w2_rows[:, :, n * DH:(n + 1) * DH]).then_inc(mlp1_w, 16)
            sp.wait_ge(w1_parts, SPLIT)
            for j in range(SPLIT):
                for i in range(SPLIT):
                    r = (j * SPLIT + i) * DES
                    sp.dma_start(w1s[r:r + DES, :], w1p[j][:, :]).then_inc(w1_stacked, 16)

            def load1(g):
                sp.wait_ge(msgs, g.slot_used())
                sp.dma_start(src_i1[g.slot][:, :],
                             src_g[bass.ds(g.at, 1), :, :].rearrange("a p t -> (a p) t")).then_inc(src1_in[g.slot], 16)
                if g.c == 0:
                    sp.wait_ge(es_parts_out, 16 * SPLIT)
                for j in range(SPLIT):
                    sp.dma_start(es_in[g.slot][j * SPLIT * DES:(j + 1) * SPLIT * DES, :],
                                 es_parts[:, bass.ds(g.at * GE, GE)]).then_inc(es_landed[g.slot], 16)

            with sp.Fori(0, n_sweeps) as p:
                sweep(sp, p, load1, lambda g: None)

            sp.wait_ge(out_set, 1)
            full = N // NB
            sp.dma_start(out[0:full * NB, :].rearrange("(p b) f -> p (b f)", b=NB),
                         out_sb[0:full, :, :].rearrange("p b f -> p (b f)")).then_inc(out_done, 16)
            sp.dma_start(out[full * NB:N, :].rearrange("(a b) f -> a (b f)", a=1),
                         out_sb[full:full + 1, 0:N - full * NB, :].rearrange("p b f -> p (b f)")).then_inc(out_done, 16)
            sp.wait_ge(out_done, 32)

        @block.gpsimd
        def _(pool):
            pool.iota(iota_i[:, :], [[1, P]], base=0, channel_multiplier=0).then_inc(iotas, 1)
            pool.iota(part_i[:, :], [[0, 1]], base=0, channel_multiplier=1).then_inc(iotas, 1)
            pool.wait_ge(iotas, 2)
            for n, rows in enumerate((w_upd[DH:P - D, :], upd_in[0:P - D, :], sums1[:, :])):
                pool.memset(rows, 0.0).then_inc(cleared, 1)
                pool.wait_ge(cleared, n + 1)
            for d in d_win:
                pool.dma_start(d[WIN:KW, :], W1m[2 * D:2 * D + DEF, :]).then_inc(ef_w, 16)
            for n in range(QUADS):
                pool.dma_start(w_src[n * D:(n + 1) * D, :], W1m_src_by_i).then_inc(w_src_in, 16)
            pool.wait_ge(sweeps_set, 1)
            n_sweeps = pool.value_load(sweeps[0:1, 0:1], min_val=1, max_val=MAX_SWEEPS)
            pool.wait_ge(src_table_out, 16)

            def gather0(g):
                if g.picks:
                    return
                pool.wait_ge(src_in[g.slot], g.filled_unpicked(16))
                pool.sem_inc(indices_seen, 1)
                for t in range(TILES):
                    pool.indirect_dma_start(
                        out=gat0[g.slot][:, t, :], out_offset=None, in_=src_table,
                        in_offset=bass.IndirectOffsetOnAxis(ap=src_i[g.slot][:, t:t + 1], axis=0),
                    ).then_inc(gathered0[g.slot], 16)

            with pool.Fori(0, n_sweeps) as p:
                sweep(pool, p, gather0, lambda g: None)

            pool.wait_ge(x1_out, 16)

            def gather1(g):
                pool.wait_ge(src1_in[g.slot], g.filled(16))
                pool.sem_inc(indices_seen, 1)
                for t in range(TILES):
                    pool.indirect_dma_start(
                        out=gat1[g.slot][:, t, :], out_offset=None, in_=x1_table,
                        in_offset=bass.IndirectOffsetOnAxis(ap=src_i1[g.slot][:, t:t + 1], axis=0),
                    ).then_inc(gathered1[g.slot], 16)

            with pool.Fori(0, n_sweeps) as p:
                sweep(pool, p, gather1, lambda g: None)

        @block.tensor
        def _(pe):
            pe.wait_ge(x_in, 16)
            pe.wait_ge(tab_w, 48)
            pe.wait_ge(tab_zero, 1)
            xt_by_b = xt1[:, :].rearrange("k (p b) -> k b p", b=NB)
            for k, (h, f) in enumerate(table_parts):
                for q in range(QUADS):
                    mm = pe.matmul(banks[k][q * QP:(q + 1) * QP, 0:HALF], w_tab[:, f * D:(f + 1) * D],
                                   xt_by_b[:, h * HB:(h + 1) * HB, q * QP:(q + 1) * QP], start=True, stop=True)
                mm.then_inc(table_ps, 1)
            pe.wait_ge(upd_w, 16 * 9)
            pe.wait_ge(table_dve, 1)
            pe.matmul(banks[0][0:DH + 1, 0:DH], w_msg_t[:, :], w_upd_a[:, :], start=True, stop=True).then_inc(upd_w_mm, 1)
            pe.wait_ge(sweeps_set, 1)
            n_sweeps = pe.value_load(sweeps[0:1, 0:1], min_val=1, max_val=MAX_SWEEPS)
            pe.wait_ge(table_dve, len(table_parts))
            pe.wait_ge(upd_w_set, 1)
            pe.wait_ge(ef_w, 16 * SLOTS)
            pe.wait_ge(w_src_in, 16 * QUADS)
            pe.wait_ge(x_cast, SPLIT)

            def pre_products(g):
                pe.wait_ge(pre_in[g.slot], g.filled(32))
                pe.wait_ge(hot_ready, g.count(0))
                pe.wait_ge(pre_sum, g.count(SLOTS - 2))
                for t in range(TILES):
                    pre_t = pre_ps[g.slot % 2][:, t * DH:(t + 1) * DH]
                    mm = pe.matmul(pre_t, hot_t[g.slot][:, t * P:(t + 1) * P], d_win[g.slot][:, :], start=True,
                                   stop=not g.picks)
                    if g.picks:
                        if t == 0:
                            pe.wait_ge(picked_set, g.sets(1))
                        mm = pe.matmul(pre_t, picked_t[:, t * P:(t + 1) * P], w_src[:, :], start=False, stop=True)
                mm.then_inc(pre_mm, 1)

            def pick_rows(g):
                pe.wait_ge(pick_ready, g.piece(0))
                if g.slot == 0:
                    pe.wait_ge(picked_set, g.sets(1))
                for b in step_blocks[g.slot]:
                    for n in range(SPLIT):
                        k = b * SPLIT + n
                        q = k % QUADS
                        mm = pe.matmul(banks[0][q * D:(q + 1) * D, :], x_parts[:, b, n, :], pick[:, b, :],
                                       start=k < QUADS, stop=k + QUADS >= NB * SPLIT)
                mm.then_inc(pick_used, 1)

            def sum0(g):
                pe.wait_ge(relu0, g.count(0))
                pe.wait_ge(hot0, g.count(1))
                pe.wait_ge(added0, g.count(0))
                for t in range(TILES):
                    mm = pe.matmul(small[g.slot % 2][0:DH + 1, 0:WIN], hid[g.slot % 2][:, t, :], hot[g.slot][:, t, :],
                                   start=t == 0, stop=t == TILES - 1)
                mm.then_inc(seg0, 1)

            def step0(g):
                if g.c >= 2:
                    sum0(g.back(2))
                pre_products(g)
                if g.c >= 1 and g.back(1).prepares:
                    pick_rows(g.back(1))

            def drain0(g):
                sum0(g.back(2))
                sum0(g.back(1))

            with pe.Fori(0, n_sweeps) as p:
                sweep(pe, p, step0, drain0)

            pe.wait_ge(added0, n_sweeps * NG + 2)
            pe.wait_ge(nodes_in, 32)
            pe.wait_ge(cleared, 3)
            for c in range(NCH):
                for k in range(2):
                    mm = pe.matmul(banks[c][k * DH:(k + 1) * DH, 0:HALF], w_upd[:, :],
                                   upd_in[:, (k * NCH + c) * HALF:(k * NCH + c + 1) * HALF], start=True, stop=True)
                mm.then_inc(upd_mm, 1)
            pe.wait_ge(w_out_set, 1)
            pe.wait_ge(upd_relu, NCH)
            for h in range(2):
                for q in range(QUADS):
                    rows = slice(q // 2 * DH, (q // 2 + 1) * DH)
                    hid_by_b = upd_hid[rows, :].rearrange("k (p b) -> k b p", b=NB)
                    mm = pe.matmul(small[h][q * QP:(q + 1) * QP, 0:HALF], w_out[rows, :],
                                   hid_by_b[:, h * HB:(h + 1) * HB, q % 2 * QP:(q % 2 + 1) * QP], start=True, stop=True)
                mm.then_inc(y_mm, 1)

            pe.wait_ge(w1_stacked, 16 * SPLIT * SPLIT)
            pe.wait_ge(mlp1_w, 16 * 4)

            def hidden1(g):
                pe.wait_ge(es_landed[g.slot], g.filled(16 * SPLIT))
                pe.wait_ge(relu1, g.count(0))
                for c in range(2):
                    mm = pe.matmul(hid_ps[:, c * GE:(c + 1) * GE], w1s[:, c * P:(c + 1) * P], es_in[g.slot][:, :],
                                   start=True, stop=True)
                mm.then_inc(hid_mm, 1)

            def weights1(g):
                pe.wait_ge(relu1, g.count(1))
                pe.wait_ge(prods, g.count(0))
                for t in range(TILES):
                    for c in range(2):
                        mm = pe.matmul(w_ps[g.slot % 2][:, t, :], hid1[g.slot % 2][:, c, t * P:(t + 1) * P],
                                       w2[:, c, :], start=c == 0, stop=c == 1)
                mm.then_inc(w_mm, 1)

            def sum1(g):
                pe.wait_ge(msgs, g.count(SLOTS))
                pe.wait_ge(hot1, g.count(1))
                pe.wait_ge(added1, g.count(0))
                for t in range(TILES):
                    mm = pe.matmul(small[g.slot % 2][t % 2 * 2 * D:(t % 2 + 1) * 2 * D, 0:WIN], msg[g.slot % 2][:, t, MUL:],
                                   hot[g.slot][:, t, :], start=t < 2, stop=t >= 2)
                mm.then_inc(seg1, 1)

            def step1(g):
                hidden1(g)
                if g.c >= 1:
                    weights1(g.back(1))
                if g.c >= 2:
                    sum1(g.back(2))

            def drain1(g):
                weights1(g.back(1))
                sum1(g.back(2))
                sum1(g.back(1))

            with pe.Fori(0, n_sweeps) as p:
                sweep(pe, p, step1, drain1)

            pe.wait_ge(added1, n_sweeps * NG + 2)
            sums_by_b = sums1[:, :].rearrange("k (p b) -> k b p", b=NB)
            for h in range(2):
                for q in range(QUADS):
                    mm = pe.matmul(banks[h][q * QP:(q + 1) * QP, 0:HALF], fold[:, :],
                                   sums_by_b[:, h * HB:(h + 1) * HB, q * QP:(q + 1) * QP], start=True, stop=True)
                mm.then_inc(fold_mm, 1)

        @block.scalar
        def _(act):
            act.dma_start(w_tab[0:D, 0:DH], W1m[0:D, :]).then_inc(tab_w, 16)
            act.dma_start(w_tab[0:D, DH:2 * DH], W1m[D:2 * D, :]).then_inc(tab_w, 16)
            act.dma_start(w_tab[D:D + 1, 0:DH], b1m.rearrange("(a n) -> a n", a=1)).then_inc(tab_w, 16)
            act.dma_start(w1f[:, :], fc_w1).then_inc(w1_in, 16)
            act.dma_start(es[:, :], es_t).then_inc(es_loaded, 16)
            act.dma_start(x_nm[:, :, :].rearrange("p b f -> p (b f)"), x_rows).then_inc(x_in_nm, 16)
            act.dma_start(w_msg_t[:, 0:DH], W2m_t).then_inc(upd_w, 16)
            act.dma_start(w_msg_t[:, DH:DH + 1], b2m.rearrange("(n a) -> n a", a=1)).then_inc(upd_w, 16)
            act.dma_start(w_upd_a[:, :], W1u[D:2 * D, :]).then_inc(upd_w, 16)
            for k in range(2):
                act.dma_start(b_upd[k * DH:(k + 1) * DH, :], b1u.rearrange("(n a) -> n a", a=1)).then_inc(upd_w, 16)
                act.dma_start(w_out[k * DH:(k + 1) * DH, :], W2u).then_inc(upd_w, 16)
            act.dma_start(b_out[:, :], b2u.partition_broadcast(P)).then_inc(upd_w, 16)
            act.dma_start(w_upd[P - D:P, :], W1u[0:D, :]).then_inc(upd_w, 16)
            def split_x(n):
                if n:
                    act.wait_ge(x_left, n)
                act.activation(x_parts[:, :, n, :], (x_rest if n else x_nm)[:, :, :], ACT.Copy).then_inc(x_cast, 1)

            def split_es(n):
                for k, cols in enumerate(es_chunks):
                    if n:
                        act.wait_ge(es_rest, (n - 1) * len(es_chunks) + k + 1)
                    act.activation(esp[n][:, cols], es[:, cols], ACT.Copy).then_inc(es_cast, 1)

            act.wait_ge(es_loaded, 16)
            split_es(0)
            act.wait_ge(x_in_nm, 16)
            split_x(0)
            act.wait_ge(table_dve, 8)
            act.dma_start(dst_table.rearrange("(p b) f -> p (b f)", b=NB),
                          tables[:, 0, :, :].rearrange("p b f -> p (b f)")).then_inc(dst_table_out, 16)
            act.dma_start(upd_in[P - D:P, :], x_t[0:D, :]).then_inc(nodes_in, 16)
            for n in range(1, SPLIT):
                split_es(n)
                split_x(n)
            act.wait_ge(cleared, 3)
            act.wait_ge(upd_w_mm, 1)
            act.activation(w_upd[0:DH + 1, :], banks[0][0:DH + 1, 0:DH], ACT.Copy).then_inc(upd_w_set, 1)
            act.wait_ge(sweeps_set, 1)
            n_sweeps = act.value_load(sweeps[0:1, 0:1], min_val=1, max_val=MAX_SWEEPS)

            def relu_0(g):
                act.wait_ge(pre_sum, g.count(SLOTS))
                act.wait_ge(seg0, g.count(0))
                act.activation(hid[g.slot % 2][:, :, 0:DH], pre[g.slot % 2][:, :, :], ACT.Relu).then_inc(relu0, 1)

            def one_hots(g, made, ready):
                act.wait_ge(ready, g.count(0))
                for t in range(TILES):
                    last = act.activation(away[:, t, :], iota[:, 0:WIN], ACT.Square,
                                          bias=neg_rel[:, bass.ds(g.at, 1), t:t + 1].rearrange("p a b -> p (a b)"))
                last.then_inc(made, 1)
                act.wait_ge(made, g.count(0))
                act.activation(hot[g.slot][:, :, :], away[:, :, :], ACT.Relu, scale=-1.0, bias=1.0).then_inc(ready, 1)

            def step0(g):
                if g.c < LEAD:
                    act.wait_ge(seg0, g.count(0))
                one_hots(g, hot_away0, hot0)
                if g.c == PICKER - 1:
                    act.wait_ge(pick_used, g.back(1).piece(STEPS))
                    act.wait_ge(pre_mm, g.count(PICKER - g.c - SLOTS))
                    act.activation(picked_t[:, :], banks[0], ACT.Copy).then_inc(picked_set, 1)
                relu_0(g)

            with act.Fori(0, n_sweeps) as p:
                act.wait_ge(windows_set, p + 1)
                sweep(act, p, step0, lambda g: None)

            act.wait_ge(es_cast, SPLIT * len(es_chunks))
            for n in range(SPLIT):
                act.dma_start(es_parts[n * DES:(n + 1) * DES, :].rearrange("f (c e) -> (f c) e", e=EC),
                              esp[n][:, :]).then_inc(es_parts_out, 16)
            act.dma_start(sh[:, :, :].rearrange("p t k -> p (t k)"), sh_tiles).then_inc(sh_loaded, 16)
            for c in range(NCH):
                act.wait_ge(upd_mm, c + 1)
                act.activation(upd_hid[:, c * HALF:(c + 1) * HALF], banks[c][:, 0:HALF], ACT.Relu,
                               bias=b_upd[:, :]).then_inc(upd_relu, 1)
            act.activation(std[:, 0:1], eps[:, :], ACT.Sqrt).then_inc(std_warm, 1)

            def norm_parts(turn):
                for h in range(2):
                    half = slice(h * HB, (h + 1) * HB)
                    act.wait_ge(centred, 2 * turn + h + 1)
                    act.activation(y[:, half, :], yy[:, half, :], ACT.Square).then_inc(squared, 1)
                for h in range(2):
                    half = slice(h * HB, (h + 1) * HB)
                    act.wait_ge(var_set, 2 * turn + h + 1)
                    act.activation(std[:, half], squares[:, half], ACT.Sqrt, scale=1.0 / D,
                                   bias=eps[:, :]).then_inc(std_set, 1)

            norm_parts(0)
            act.wait_ge(x1_set, 1)
            act.dma_start(x1_table.rearrange("(p b) f -> p (b f)", b=NB),
                          x1[:, :, :].rearrange("p b f -> p (b f)")).then_inc(x1_out, 16)

            act.wait_ge(sh_loaded, 16)
            act.activation(sh8[:, :, 0:1], sh[:, :, 0:1], ACT.Copy, scale=C_S).then_inc(sh_scaled, 1)
            act.activation(sh8[:, :, 1:DEA], sh[:, :, 1:DEA], ACT.Copy, scale=C_S3).then_inc(sh_scaled, 1)
            act.activation(sh8[:, :, DEA:2 * DEA], sh[:, :, :], ACT.Copy, scale=C_V).then_inc(sh_scaled, 1)

            def relu_1(g):
                act.wait_ge(hid_mm, g.count(0))
                act.wait_ge(w_mm, g.count(0))
                act.activation(hid1[g.slot % 2][:, :, :].rearrange("p c e -> p (c e)"), hid_ps[:, :],
                               ACT.Relu).then_inc(relu1, 1)

            def hot_1(g):
                act.wait_ge(seg1, g.slot_used())
                one_hots(g, hot_away, hot1)

            def scale_1(g):
                act.wait_ge(gathered1[g.slot], g.filled(16 * TILES))
                act.wait_ge(prods, g.count(0))
                act.activation(feat[g.slot % 2][:, :, 0:MUL], gat1[g.slot][:, :, 0:MUL], ACT.Copy)
                for t in range(TILES):
                    last = act.activation(feat[g.slot % 2][:, t, 2 * MUL:6 * MUL], gat1[g.slot][:, t, :], ACT.Copy,
                                          scale=sh8[:, bass.ds(g.at * TILES + t, 1), 0:1].rearrange("p a b -> p (a b)"))
                last.then_inc(scaled_feats, 1)

            def step1(g):
                relu_1(g)
                hot_1(g)
                scale_1(g)

            with act.Fori(0, n_sweeps) as p:
                act.wait_ge(windows_set, n_sweeps + p + 2)
                sweep(act, p, step1, lambda g: None)

            norm_parts(1)

        @block.vector
        def _(dve):
            done = [0]

            def link(ins):
                done[0] += 1
                ins.then_inc(dve_chain, 1)
                dve.wait_ge(dve_chain, done[0])

            for s, n in ((pre_sum, SLOTS), (added0, 2), (seg0, 2), (relu1, 1), (prods, 2), (msgs, SLOTS),
                         (added1, 2), (w_mm, 2), (seg1, SLOTS), (hot0, 1), (hot1, 1), (pick_used, STEPS),
                         (picked_set, 1), (rel_set, 1)):
                dve.sem_inc(s, n)
            link(dve.memset(w_tab[D:D + 1, DH:2 * DH], 0.0))
            dve.memset(shift[:, :], 0.0)
            dve.memset(eps[:, :], EPS).then_inc(tab_zero, 1)
            dve.wait_ge(dst_grouped, 16)
            dve.tensor_reduce(ranges[:, 0:1], dst_g[:, :], AX_X, ALU.min).then_inc(ranges_set, 1)
            link(dve.scalar_tensor_tensor(out=dst_in[:, :], in0=dst_g[:, :], scalar=float(NO_DST), in1=dst_g[:, :],
                                          op0=ALU.is_lt, op1=ALU.mult))
            dve.tensor_reduce(ranges[:, 1:2], dst_in[:, :], AX_X, ALU.max).then_inc(ranges_set, 1)
            dve.wait_ge(iotas, 2)
            dve.tensor_copy(iota[:, :], iota_i[:, :])
            link(dve.tensor_copy(part[:, :], part_i[:, :]))

            dve.wait_ge(w1_in, 16)
            for n in range(SPLIT):
                dve.tensor_copy(w1p[n][:, :], w1f[:, :]).then_inc(w1_parts, 1)
                if n < SPLIT - 1:
                    dve.wait_ge(w1_parts, n + 1)
                    link(dve.tensor_tensor(w1f[:, :], w1f[:, :], w1p[n][:, :], ALU.subtract))

            def evacuate(k):
                h, f = table_parts[k]
                dve.wait_ge(table_ps, k + 1)
                nc.vector.transpose(tables[:, f // 2, h * HB:(h + 1) * HB, f % 2 * D:(f % 2 + 1) * D],
                                    banks[k][:, 0:HALF].rearrange("p (b f) -> p b f", f=D)).then_inc(table_dve, 1)

            for k in range(4):
                evacuate(k)
            dve.wait_ge(range_row_in, 16)
            link(dve.tensor_tensor(spans[:, :], range_row[:, :, 1], range_row[:, :, 0], ALU.subtract))
            link(dve.tensor_reduce(span[:, :], spans[:, :], AX_X, ALU.max))
            link(dve.tensor_scalar(reached[:, :], iota[0:1, 0:MAX_SWEEPS], float(WIN), span[:, 0:1], ALU.mult,
                                   ALU.is_le))
            link(dve.tensor_reduce(windows[:, :], reached[:, :], AX_X, ALU.add))
            dve.tensor_copy(sweeps[:, :], windows[:, :]).then_inc(sweeps_set, 1)

            dve.wait_ge(range_all_in, 16)
            dve.wait_ge(dst_by_tile, 16)

            def set_windows(sweep_no):
                if not isinstance(sweep_no, int):
                    dve.wait_ge(shifted, sweep_no)
                dve.tensor_scalar(base[:, :], range_all[:, :, 0], shift[:, 0:1], None,
                                  ALU.add).then_inc(window_base, 1)
                dve.wait_ge(window_base, sweep_no + 1)
                dve.tensor_scalar(node_of[:, :], base[:, :], part[:, 0:1], None, ALU.add)
                dve.tensor_scalar(base_at[:, :], base[0:1, :], float(OFF_TABLE), None, ALU.min)
                first = base[:, :, None].to_broadcast([P, NG, TILES])
                dve.tensor_tensor(neg_rel[:, :, :], first, dst_l[:, :, :], ALU.subtract).then_inc(windows_set, 1)
                dve.wait_ge(windows_set, sweep_no + 1)
                dve.tensor_scalar(shift[:, :], shift[:, :], float(WIN), None, ALU.add).then_inc(shifted, 1)

            set_windows(0)
            for k in range(4, 8):
                evacuate(k)
            link(dve.memset(hid[0][:, :, DH:DH + 1], 1.0))
            link(dve.memset(hid[1][:, :, DH:DH + 1], 1.0))
            for n in range(SPLIT - 1):
                for k, cols in enumerate(es_chunks):
                    dve.wait_ge(es_cast, n * len(es_chunks) + k + 1)
                    dve.tensor_tensor(es[:, cols], es[:, cols], esp[n][:, cols], ALU.subtract).then_inc(es_rest, 1)
                dve.wait_ge(x_cast, n + 1)
                dve.tensor_tensor(x_rest[:, :, :], (x_rest if n else x_nm)[:, :, :], x_parts[:, :, n, :],
                                  ALU.subtract).then_inc(x_left, 1)
            dve.wait_ge(upd_w, 16 * 9)
            link(dve.tensor_reduce(w_mean[:, :], w_out[:, :], AX_X, ALU.add))
            dve.scalar_tensor_tensor(out=w_out[:, :], in0=w_mean[:, 0:1].to_broadcast([P, D]), scalar=-1.0 / D,
                                     in1=w_out[:, :], op0=ALU.mult, op1=ALU.add).then_inc(w_out_set, 1)
            link(dve.tensor_scalar(part_node[:, :], part[:, :], float(NB), None, ALU.mult))
            n_sweeps = dve.value_load(sweeps[0:1, 0:1], min_val=1, max_val=MAX_SWEEPS)

            def pick_hots(g):
                if g.slot == 0:
                    dve.wait_ge(srcb_in, g.sets(1) * 16)
                    dve.tensor_scalar(src_rel[:, :], src_b[:, :], part_node[:, 0:1], None,
                                      ALU.subtract).then_inc(rel_set, 1)
                    dve.wait_ge(rel_set, g.sets(2))
                dve.wait_ge(pick_used, g.piece(0))
                for b in step_blocks[g.slot]:
                    last = dve.tensor_scalar(pick[:, b, :], src_rel[:, :], float(b), None, ALU.is_equal)
                last.then_inc(pick_ready, 1)

            def one_hots(g):
                dve.wait_ge(dstb_in[g.slot], g.filled(16))
                dve.tensor_scalar(hot_t[g.slot][0:WIN, :], dst_b[g.slot][0:WIN, :], node_of[0:WIN, bass.ds(g.at, 1)],
                                  None, ALU.is_equal).then_inc(hot_ready, 1)

            def sum_pre(g):
                dve.wait_ge(pre_mm, g.count(0))
                into = pre[g.slot % 2][:, :, :].rearrange("p t f -> p (t f)")
                if g.picks:
                    dve.tensor_copy(into, pre_ps[g.slot % 2]).then_inc(pre_sum, 1)
                else:
                    dve.wait_ge(gathered0[g.slot], g.filled_unpicked(16 * TILES))
                    dve.tensor_tensor(into, pre_ps[g.slot % 2], gat0[g.slot][:, :, :].rearrange("p t f -> p (t f)"),
                                      ALU.add).then_inc(pre_sum, 1)

            def add_to_nodes(g, first, acc, rows, summed, credit, added):
                dve.wait_ge(summed, g.count(credit))
                dve.wait_ge(added, g.count(1))
                there = acc[0:rows, bass.ds(first, WIN)]
                dve.tensor_tensor(there, there, small[g.slot % 2][0:rows, 0:WIN], ALU.add).then_inc(added, 1)

            def add0(g):
                first = dve.value_load(base_at[0:1, bass.ds(g.at, 1)], min_val=0, max_val=OFF_TABLE)
                add_to_nodes(g, first, upd_in, DH + 1, seg0, 2, added0)

            def step0(g):
                one_hots(g)
                if g.c >= 1:
                    sum_pre(g.back(1))
                if g.prepares:
                    pick_hots(g)
                if g.c >= 2:
                    add0(g.back(2))

            def drain0(g):
                add0(g.back(2))
                sum_pre(g.back(1))
                add0(g.back(1))

            def next0(g):
                drain0(g)
                set_windows(g.p + 1)

            with dve.Fori(0, n_sweeps) as p:
                sweep(dve, p, step0, next0)

            def centre(rows):
                link(dve.tensor_reduce(total[:, :], rows[:, :, :], AX_X, ALU.add))
                link(dve.scalar_tensor_tensor(out=x_cen[:, :, :], in0=total[:, :, None].to_broadcast([P, NB, D]),
                                              scalar=-1.0 / D, in1=rows[:, :, :], op0=ALU.mult, op1=ALU.add))

            def layernorm(src, src_ready, turn, normed):
                halves = [slice(h * HB, (h + 1) * HB) for h in range(2)]
                for h, half in enumerate(halves):
                    dve.wait_ge(src_ready, h + 1)
                    link(nc.vector.transpose(y[:, half, :], src[h][:, 0:HALF].rearrange("p (b f) -> p b f", f=D)))
                    dve.tensor_tensor(yy[:, half, :], y[:, half, :], x_cen[:, half, :], ALU.add).then_inc(centred, 1)
                for h, half in enumerate(halves):
                    dve.wait_ge(squared, 2 * turn + h + 1)
                    dve.tensor_reduce(squares[:, half], y[:, half, :], AX_X, ALU.add).then_inc(var_set, 1)
                for h, half in enumerate(halves):
                    dve.wait_ge(std_set, 2 * turn + h + 1)
                    link(dve.reciprocal(rstd[:, half], std[:, half]))
                    last = normed(half, rstd[:, half])
                return last

            def to_x1(half, r):
                return dve.tensor_tensor(x1[:, half, :], yy[:, half, :], r[:, :, None].to_broadcast([P, HB, D]),
                                         ALU.mult)

            dve.wait_ge(nodes_in, 32)
            link(dve.tensor_tensor(x_nm[:, :, :], x_nm[:, :, :], b_out[:, None, :].to_broadcast([P, NB, D]), ALU.add))
            centre(x_nm)
            layernorm(small, y_mm, 0, to_x1).then_inc(x1_set, 1)
            dve.wait_ge(x1_set, 1)
            centre(x1)
            link(dve.memset(shift[:, :], 0.0))
            set_windows(n_sweeps + 1)
            dve.wait_ge(sh_scaled, 3)

            def times_v2(g):
                dve.wait_ge(vec_sums, g.count(0))
                m = msg[g.slot % 2]
                h = sh8[:, bass.ds(g.at * TILES, TILES), DEA + 1:2 * DEA]
                dve.tensor_tensor(m[:, :, 6 * MUL:9 * MUL].rearrange("p t (i w) -> p t i w", i=3),
                                  m[:, :, None, 0:MUL].to_broadcast([P, TILES, 3, MUL]),
                                  h[:, :, :, None].to_broadcast([P, TILES, 3, MUL]), ALU.mult).then_inc(msgs, 1)

            def step1(g):
                f, m, w, rows = feat[g.slot % 2], msg[g.slot % 2], w_ps[g.slot % 2], gat1[g.slot]
                v2 = sh8[:, bass.ds(g.at * TILES, TILES), 1:DEA]
                if g.c >= 2:
                    first = dve.value_load(base_at[0:1, bass.ds(g.back(2).at, 1)], min_val=0, max_val=OFF_TABLE)
                dve.wait_ge(gathered1[g.slot], g.filled(16 * TILES))
                dve.tensor_tensor(vv[:, :, :, :], rows[:, :, MUL:D].rearrange("p t (i u) -> p t i u", i=3),
                                  v2[:, :, :, None].to_broadcast([P, TILES, 3, MUL]), ALU.mult).then_inc(vec_feats, 1)
                if g.c >= 1:
                    times_v2(g.back(1))
                dve.wait_ge(vec_feats, g.count(0))
                dve.tensor_reduce(f[:, :, MUL:2 * MUL], vv[:, :, :, :].rearrange("p t i u -> p t u i"), AX_X,
                                  ALU.add).then_inc(scal_feats, 1)
                dve.wait_ge(w_mm, g.count(2))
                dve.wait_ge(scaled_feats, g.count(0))
                dve.tensor_tensor(terms[:, :, 3:6, :].rearrange("p t i (u w) -> p t i u w", w=MUL),
                                  w[:, :, None, 192:256].rearrange("p t i (u w) -> p t i u w", w=MUL)
                                  .to_broadcast([P, TILES, 3, MUL, MUL]),
                                  f[:, :, 3 * MUL:6 * MUL].rearrange("p t (i u) -> p t i u", i=3)[:, :, :, :, None]
                                  .to_broadcast([P, TILES, 3, MUL, MUL]), ALU.mult)
                dve.wait_ge(scal_feats, g.count(0))
                dve.tensor_tensor(terms[:, :, 0:3, :].rearrange("p t j (u w) -> p t (j u) w", w=MUL),
                                  w[:, :, 0:192].rearrange("p t (u w) -> p t u w", w=MUL),
                                  f[:, :, 0:3 * MUL, None].to_broadcast([P, TILES, 3 * MUL, MUL]),
                                  ALU.mult).then_inc(prods, 1)
                if g.c >= 2:
                    add_to_nodes(g.back(2), first, sums1, P, seg1, SLOTS, added1)
                dve.wait_ge(prods, g.count(2))
                dve.tensor_reduce(m[:, :, 0:6 * MUL].rearrange("p t (j w) -> p t j w", w=MUL),
                                  terms[:, :, :, :].rearrange("p t j (u w) -> p t j w u", w=MUL), AX_X,
                                  ALU.add).then_inc(vec_sums, 1)

            def drain1(g):
                times_v2(g.back(1))
                for n in (2, 1):
                    first = dve.value_load(base_at[0:1, bass.ds(g.back(n).at, 1)], min_val=0, max_val=OFF_TABLE)
                    add_to_nodes(g.back(n), first, sums1, P, seg1, SLOTS, added1)
                set_windows(n_sweeps + g.p + 2)

            with dve.Fori(0, n_sweeps) as p:
                sweep(dve, p, step1, drain1)

            def to_out(half, r):
                dve.tensor_tensor(out_sb[:, half, 0:MUL], yy[:, half, 0:MUL], r[:, :, None].to_broadcast([P, HB, MUL]),
                                  ALU.mult)
                return dve.tensor_tensor(out_sb[:, half, MUL:D].rearrange("p b (u i) -> p b i u", i=3),
                                         yy[:, half, MUL:D].rearrange("p b (i u) -> p b i u", i=3),
                                         r[:, :, None, None].to_broadcast([P, HB, 3, MUL]), ALU.mult)

            layernorm(banks, fold_mm, 1, to_out).then_inc(out_set, 1)


def kernel(x, src, dst, edge_attr_16, edge_attr_4, edge_attr_8, L0_gnn_W1m, L0_gnn_b1m, L0_gnn_W2m, L0_gnn_b2m,
           L0_gnn_W1u, L0_gnn_b1u, L0_gnn_W2u, L0_gnn_b2u, L1_gnn_fc_w1, L1_gnn_fc_w2):
    import concourse.bacc as bacc
    from concourse.bass_utils import run_bass_kernel_spmd

    def padded(a, rows, fill=0):
        a = np.asarray(a)
        full = np.full((rows,) + a.shape[1:], fill, a.dtype)
        full[:a.shape[0]] = a
        return full

    xp = padded(x, NT)
    dp = padded(dst, EP, NO_DST)
    by_i = np.concatenate([np.arange(MUL), MUL + np.arange(3 * MUL).reshape(MUL, 3).T.ravel()])
    fold = np.full((2, 2 * D, D), -1 / D, np.float32)
    for w in range(MUL):
        fold[:, [w, MUL + w], w] += 1
        for i in range(3):
            fold[:, [(2 + i) * MUL + w, (5 + i) * MUL + w], (1 + i) * MUL + w] += 1
    arrays = {
        "x_t": np.concatenate([xp.T, np.ones((1, NT), xp.dtype)]),
        "x_rows": np.ascontiguousarray(xp[:, by_i]).reshape(P, NB * D),
        "src_g": np.ascontiguousarray(padded(src, EP).reshape(NG, TILES, P).transpose(0, 2, 1)),
        "src_row": padded(src, EP),
        "dst_row": dp,
        "dst_tiles": np.ascontiguousarray(dp.reshape(NG * TILES, P).T),
        "ef_t": np.ascontiguousarray(padded(edge_attr_16, EP).T),
        "sh_tiles": np.ascontiguousarray(
            padded(edge_attr_4, EP).reshape(NG * TILES, P, DEA).transpose(1, 0, 2)).reshape(P, -1),
        "es_t": np.ascontiguousarray(padded(edge_attr_8, EP).T).reshape(P, EC),
        "W1m": np.asarray(L0_gnn_W1m), "b1m": np.asarray(L0_gnn_b1m),
        "W1m_src_by_i": np.ascontiguousarray(np.asarray(L0_gnn_W1m)[D + by_i]),
        "W2m_t": np.ascontiguousarray(np.asarray(L0_gnn_W2m).T), "b2m": np.asarray(L0_gnn_b2m),
        "W1u": np.asarray(L0_gnn_W1u), "b1u": np.asarray(L0_gnn_b1u),
        "W2u": np.ascontiguousarray(np.asarray(L0_gnn_W2u)[:, by_i]),
        "b2u": np.ascontiguousarray(np.asarray(L0_gnn_b2u)[by_i]),
        "fc_w1": np.asarray(L1_gnn_fc_w1), "fc_w2": np.asarray(L1_gnn_fc_w2),
        "fold_rows": fold.reshape(P, D),
    }
    nc = bacc.Bacc("TRN2", target_bir_lowering=False, num_devices=1)
    ins = {n: nc.dram_tensor(f"in_{n}", a.shape, mybir.dt.from_np(a.dtype), kind="ExternalInput").ap()
           for n, a in arrays.items()}
    out = nc.dram_tensor("out_x", (N, D), F32, kind="ExternalOutput").ap()
    gnn_program(nc, **ins, out=out)
    r = run_bass_kernel_spmd(nc, [{f"in_{n}": a for n, a in arrays.items()}], core_ids=[0])
    return r.results[0]["out_x"]
```
